# Optimizing a Trainium2 kernel written in Bass

```python
import numpy as np
import jax
import jax.numpy as jnp

def _softmax(x, axis=-1):
    return jax.nn.softmax(x, axis=axis)

def _gelu(x):
    return jax.nn.gelu(x, approximate=True)

def _silu(x):
    return jax.nn.silu(x)

def _sigmoid(x):
    return jax.nn.sigmoid(x)

def _layernorm(x, axis=-1, eps=1e-05):
    m = jnp.mean(x, axis=axis, keepdims=True)
    v = jnp.var(x, axis=axis, keepdims=True)
    return (x - m) / jnp.sqrt(v + eps)

def _scatter_add(tgt, idx, src, axis=0):
    return tgt.at[idx].add(src)

def _segment_sum(src, seg, n):
    return jax.ops.segment_sum(src, seg, n)
kernel_name = 'mk_prb_d2_jaxref_r4_cbd3ce'

def setup_inputs(seed: int=0):
    np.random.seed(seed)
    _w = jnp.asarray

    def _L0_attn_setup():
        import jax, jax.numpy as jnp
        import numpy as np
        B, S, D, K = (4, 1024, 256, 64)
        key = jax.random.key(seed)
        kx, kq, kk, kv, ko = jax.random.split(key, 5)
        scale = 1.0 / np.sqrt(D)
        return {'x': jax.random.normal(kx, (B, S, D), dtype=jnp.float32), 'Wq': jax.random.uniform(kq, (K, D), dtype=jnp.float32, minval=-scale, maxval=scale), 'Wk': jax.random.uniform(kk, (K, D), dtype=jnp.float32, minval=-scale, maxval=scale), 'Wv': jax.random.uniform(kv, (K, D), dtype=jnp.float32, minval=-scale, maxval=scale), 'Wo': jax.random.uniform(ko, (D, K), dtype=jnp.float32, minval=-1.0 / np.sqrt(K), maxval=1.0 / np.sqrt(K))}
    _L0_attn_in = _L0_attn_setup()

    def _L0_ffn_setup():
        import jax, jax.numpy as jnp
        import numpy as np
        EPS = 1e-08

        def _ternary_linear(x, w):
            alpha = jnp.mean(jnp.abs(w))
            w_t = jnp.sign(w) * (jnp.abs(w) > 0.5 * alpha).astype(w.dtype)
            w_q = w + jax.lax.stop_gradient(w_t - w)
            d = x.shape[-1]
            rms = jnp.sqrt(jnp.sum(x * x, axis=-1, keepdims=True)) / jnp.sqrt(jnp.asarray(d, x.dtype))
            x_norm = x / (rms + EPS)
            return jnp.einsum('bsd,fd->bsf', x_norm, w_q)
        key = jax.random.key(seed)
        k1, k2, k3 = jax.random.split(key, 3)
        d_model, d_ff = (256, 1024)
        B, S = (4, 1024)
        x = jax.random.normal(k1, (B, S, d_model), dtype=jnp.float32)
        w_up = jax.random.normal(k2, (d_ff, d_model), dtype=jnp.float32) * 0.02
        w_down = jax.random.normal(k3, (d_model, d_ff), dtype=jnp.float32) * 0.02
        return {'x': x, 'w_up': w_up, 'w_down': w_down}
    _L0_ffn_in = _L0_ffn_setup()

    def _L1_attn_setup():
        import jax, jax.numpy as jnp
        import numpy as np
        from jax import lax
        B, T, C = (4, 256, 256)
        N = 64
        H = C // N
        D_MIX, D_DECAY, D_LORA, D_GATE = (32, 64, 16, 128)
        EPS = 0.00064

        def wkv7(r, w, k, v, a, b):
            B_, T_, C_ = r.shape
            resh = lambda t: t.reshape(B_, T_, H, N).transpose(1, 0, 2, 3)
            rT, kT, vT, aT, bT = map(resh, (r, k, v, a, b))
            dT = jnp.exp(resh(w))

            def step(S, inp):
                rt, dt, kt, vt, at, bt = inp
                sa = jnp.einsum('bhij,bhj->bhi', S, at)
                S = S * dt[:, :, None, :] + sa[..., None] * bt[:, :, None, :] + vt[..., None] * kt[:, :, None, :]
                y = jnp.einsum('bhij,bhj->bhi', S, rt)
                return (S, y)
            S0 = jnp.zeros((B_, H, N, N), r.dtype)
            _, ys = lax.scan(step, S0, (rT, dT, kT, vT, aT, bT))
            return ys.transpose(1, 0, 2, 3).reshape(B_, T_, C_)

        def _forward(x, time_maa_x, time_maa_rg, time_maa_wa, time_maa_k, time_maa_v, time_maa_w1, time_maa_w2, time_decay, time_decay_w1, time_decay_w2, time_faaaa, time_aaaaa, time_aaa_w1, time_aaa_w2, time_kkk_w1, time_kkk_w2, gate_w1, gate_w2, ma_w1, ma_w2, time_misc_a, mk_w1, mk_w2, time_misc_k, w_receptance, w_key, w_value, w_output, ln_w, ln_b):
            B_, T_, C_ = x.shape
            xprev = jnp.concatenate([jnp.zeros_like(x[:, :1]), x[:, :-1]], axis=1)
            xx = xprev - x
            mix_in = jnp.tanh((x + xx * time_maa_x) @ time_maa_w1)
            mix = jnp.einsum('btfd,fdc->fbtc', mix_in.reshape(B_, T_, 4, D_MIX), time_maa_w2)
            mrg, mwa, mk_, mv_ = (mix[0], mix[1], mix[2], mix[3])
            xrg = x + xx * (time_maa_rg + mrg)
            xwa = x + xx * (time_maa_wa + mwa)
            xk = x + xx * (time_maa_k + mk_)
            xv = x + xx * (time_maa_v + mv_)
            r = xrg @ w_receptance.T
            w = -jax.nn.softplus(-(time_decay + jnp.tanh(xwa @ time_decay_w1) @ time_decay_w2)) - 0.5
            k = xk @ w_key.T
            v = xv @ w_value.T
            g = jnp.tanh(xrg @ gate_w1) @ gate_w2
            kk = k + jnp.tanh(xk @ time_kkk_w1) @ time_kkk_w2
            kk4 = kk.reshape(B_, T_, H, N)
            kk4 = kk4 / jnp.maximum(jnp.linalg.norm(kk4, axis=-1, keepdims=True), 1e-12)
            kk = kk4.reshape(B_, T_, C_)
            a = jax.nn.sigmoid(time_aaaaa + xwa @ time_aaa_w1 @ time_aaa_w2)
            ma = jax.nn.sigmoid(time_misc_a + xwa @ ma_w1 @ ma_w2)
            k = k * ma + k * a * (1.0 - ma)
            mk2 = jax.nn.sigmoid(time_misc_k + xk @ mk_w1 @ mk_w2)
            k = k * jnp.exp(jnp.minimum(w * mk2, 0.0))
            y = wkv7(r, w, k, v, -kk, kk * a)
            yh = y.reshape(B_ * T_, H, N)
            mu = yh.mean(-1, keepdims=True)
            var = yh.var(-1, keepdims=True)
            yh = (yh - mu) * lax.rsqrt(var + EPS)
            y = (yh.reshape(B_ * T_, C_) * ln_w + ln_b).reshape(B_, T_, C_)
            rr = r.reshape(B_, T_, H, N)
            kr = k.reshape(B_, T_, H, N)
            vr = v.reshape(B_, T_, H, N)
            y = y + ((rr * kr * time_faaaa).sum(-1, keepdims=True) * vr).reshape(B_, T_, C_)
            return y * g @ w_output.T
        key = jax.random.key(seed)
        ks = iter(jax.random.split(key, 48))
        rn = lambda shape, s=1.0: jax.random.normal(next(ks), shape, dtype=jnp.float32) * s
        un = lambda shape, lo, hi: jax.random.uniform(next(ks), shape, minval=lo, maxval=hi, dtype=jnp.float32)
        p = {'x': rn((B, T, C))}
        for nm in ('time_maa_x', 'time_maa_rg', 'time_maa_wa', 'time_maa_k', 'time_maa_v'):
            p[nm] = un((1, 1, C), 0.0, 1.0)
        p['time_maa_w1'] = rn((C, 4 * D_MIX), 0.01)
        p['time_maa_w2'] = rn((4, D_MIX, C), 0.05)
        p['time_decay'] = un((1, 1, C), -6.5, -1.0) + 0.5
        p['time_decay_w1'] = rn((C, D_DECAY), 0.01)
        p['time_decay_w2'] = rn((D_DECAY, C), 0.05)
        p['time_faaaa'] = rn((1, 1, H, N), 0.1)
        p['time_aaaaa'] = jnp.zeros((1, 1, C), jnp.float32)
        p['time_aaa_w1'] = rn((C, D_LORA), 0.01)
        p['time_aaa_w2'] = rn((D_LORA, C), 0.05)
        p['time_kkk_w1'] = rn((C, D_LORA), 0.01)
        p['time_kkk_w2'] = rn((D_LORA, C), 0.05)
        p['gate_w1'] = rn((C, D_GATE), 0.05)
        p['gate_w2'] = rn((D_GATE, C), 0.05)
        p['ma_w1'] = rn((C, D_LORA), 0.01)
        p['ma_w2'] = rn((D_LORA, C), 0.05)
        p['time_misc_a'] = jnp.zeros((1, 1, C), jnp.float32)
        p['mk_w1'] = rn((C, D_LORA), 0.01)
        p['mk_w2'] = rn((D_LORA, C), 0.05)
        p['time_misc_k'] = jnp.zeros((1, 1, C), jnp.float32)
        s = 0.5 / C ** 0.5
        p['w_receptance'] = un((C, C), -s, s)
        p['w_key'] = un((C, C), -0.1 * s, 0.1 * s)
        p['w_value'] = un((C, C), -s, s)
        p['w_output'] = rn((C, C), 0.02)
        p['ln_w'] = jnp.ones((C,), jnp.float32)
        p['ln_b'] = jnp.zeros((C,), jnp.float32)
        return p
    _L1_attn_in = _L1_attn_setup()

    def _L1_ffn_setup():
        import jax, jax.numpy as jnp
        import numpy as np
        import math
        B, T, D, H, E, TOPK, CAPF = (4, 512, 256, 16, 8, 2, 2.0)
        HD = D // H

        def layernorm(x, g, b, eps=1e-05):
            m = jnp.mean(x, -1, keepdims=True)
            v = jnp.mean(jnp.square(x - m), -1, keepdims=True)
            return (x - m) * jax.lax.rsqrt(v + eps) * g + b

        def block_forward(x, ln1_g, ln1_b, Wqkv, Wproj, ln2_g, ln2_b, Wgate, W1, b1, W2, b2):
            Bb, Tt, d = x.shape
            hd = HD
            half = hd // 2
            h = layernorm(x, ln1_g, ln1_b)
            qkv = (h @ Wqkv).reshape(Bb, Tt, H, 3 * hd)
            q, k, v = (qkv[..., :hd], qkv[..., hd:2 * hd], qkv[..., 2 * hd:])
            inv_freq = 1.0 / 10000.0 ** (jnp.arange(0, hd, 2, dtype=jnp.float32) / hd)
            ang = jnp.arange(Tt, dtype=jnp.float32)[:, None] * inv_freq
            sin = jnp.sin(ang)[None, :, None, :].astype(x.dtype)
            cos = jnp.cos(ang)[None, :, None, :].astype(x.dtype)

            def rope(t):
                t1, t2 = (t[..., :half], t[..., half:])
                return jnp.concatenate([t1 * cos - t2 * sin, t1 * sin + t2 * cos], -1)
            q, k = (rope(q), rope(k))
            scores = jnp.einsum('bqhd,bkhd->bhqk', q, k) / math.sqrt(hd)
            causal = jnp.tril(jnp.ones((Tt, Tt), dtype=bool))
            scores = jnp.where(causal, scores, jnp.asarray(-1000000000.0, scores.dtype))
            probs = jax.nn.softmax(scores, axis=-1)
            attn = jnp.einsum('bhqk,bkhd->bqhd', probs, v).reshape(Bb, Tt, d) @ Wproj
            x = x + attn
            h2 = layernorm(x, ln2_g, ln2_b)
            flat = h2.reshape(-1, d)
            N = flat.shape[0]
            capacity = int(math.ceil(CAPF * N / E))
            gates = jax.nn.softmax((flat @ Wgate).astype(jnp.float32), -1).astype(flat.dtype)
            _, top_inds = jax.lax.top_k(gates, TOPK)
            mask = jnp.zeros((N, E), dtype=bool).at[jnp.arange(N)[:, None], top_inds].set(True)
            pos = jnp.cumsum(mask.astype(jnp.int32), axis=0) * mask - 1
            keep = (pos < capacity) & mask
            t_flat = jnp.repeat(jnp.arange(N), TOPK)
            e_flat = top_inds.reshape(-1)
            p = pos[t_flat, e_flat]
            kp = keep[t_flat, e_flat]
            p_eff = jnp.where(kp, p, capacity)
            exp_in = jnp.zeros((E, capacity, d), flat.dtype).at[e_flat, p_eff].set(flat[t_flat], mode='drop')
            hmid = jax.nn.gelu(jnp.einsum('ecd,edf->ecf', exp_in, W1) + b1[:, None, :], approximate=False)
            exp_out = jnp.einsum('ecf,efd->ecd', hmid, W2) + b2[:, None, :]
            gate = gates[t_flat, e_flat] * kp.astype(flat.dtype)
            p_g = jnp.minimum(p_eff, capacity - 1)
            moe = jnp.zeros((N, d), flat.dtype).at[t_flat].add(exp_out[e_flat, p_g] * gate[:, None])
            return x + moe.reshape(Bb, Tt, d)
        key = jax.random.key(seed)
        ks = jax.random.split(key, 8)
        s = 0.02
        return {'x': jax.random.normal(ks[0], (B, T, D), jnp.float32), 'ln1_g': jnp.ones((D,), jnp.float32), 'ln1_b': jnp.zeros((D,), jnp.float32), 'Wqkv': jax.random.normal(ks[1], (D, 3 * D), jnp.float32) * s, 'Wproj': jax.random.normal(ks[2], (D, D), jnp.float32) * s, 'ln2_g': jnp.ones((D,), jnp.float32), 'ln2_b': jnp.zeros((D,), jnp.float32), 'Wgate': jax.random.normal(ks[3], (D, E), jnp.float32) * s, 'W1': jax.random.normal(ks[4], (E, D, 4 * D), jnp.float32) * s, 'b1': jnp.zeros((E, 4 * D), jnp.float32), 'W2': jax.random.normal(ks[5], (E, 4 * D, D), jnp.float32) * s, 'b2': jnp.zeros((E, D), jnp.float32)}
    _L1_ffn_in = _L1_ffn_setup()
    _d = {'L0_attn_x': _L0_attn_in['x'], 'L0_attn_Wq': _L0_attn_in['Wq'], 'L0_attn_Wk': _L0_attn_in['Wk'], 'L0_attn_Wv': _L0_attn_in['Wv'], 'L0_attn_Wo': _L0_attn_in['Wo'], 'L0_ffn_w_up': _L0_ffn_in['w_up'], 'L0_ffn_w_down': _L0_ffn_in['w_down'], 'L1_attn_time_maa_x': _L1_attn_in['time_maa_x'], 'L1_attn_time_maa_rg': _L1_attn_in['time_maa_rg'], 'L1_attn_time_maa_wa': _L1_attn_in['time_maa_wa'], 'L1_attn_time_maa_k': _L1_attn_in['time_maa_k'], 'L1_attn_time_maa_v': _L1_attn_in['time_maa_v'], 'L1_attn_time_maa_w1': _L1_attn_in['time_maa_w1'], 'L1_attn_time_maa_w2': _L1_attn_in['time_maa_w2'], 'L1_attn_time_decay': _L1_attn_in['time_decay'], 'L1_attn_time_decay_w1': _L1_attn_in['time_decay_w1'], 'L1_attn_time_decay_w2': _L1_attn_in['time_decay_w2'], 'L1_attn_time_faaaa': _L1_attn_in['time_faaaa'], 'L1_attn_time_aaaaa': _L1_attn_in['time_aaaaa'], 'L1_attn_time_aaa_w1': _L1_attn_in['time_aaa_w1'], 'L1_attn_time_aaa_w2': _L1_attn_in['time_aaa_w2'], 'L1_attn_time_kkk_w1': _L1_attn_in['time_kkk_w1'], 'L1_attn_time_kkk_w2': _L1_attn_in['time_kkk_w2'], 'L1_attn_gate_w1': _L1_attn_in['gate_w1'], 'L1_attn_gate_w2': _L1_attn_in['gate_w2'], 'L1_attn_ma_w1': _L1_attn_in['ma_w1'], 'L1_attn_ma_w2': _L1_attn_in['ma_w2'], 'L1_attn_time_misc_a': _L1_attn_in['time_misc_a'], 'L1_attn_mk_w1': _L1_attn_in['mk_w1'], 'L1_attn_mk_w2': _L1_attn_in['mk_w2'], 'L1_attn_time_misc_k': _L1_attn_in['time_misc_k'], 'L1_attn_w_receptance': _L1_attn_in['w_receptance'], 'L1_attn_w_key': _L1_attn_in['w_key'], 'L1_attn_w_value': _L1_attn_in['w_value'], 'L1_attn_w_output': _L1_attn_in['w_output'], 'L1_attn_ln_w': _L1_attn_in['ln_w'], 'L1_attn_ln_b': _L1_attn_in['ln_b'], 'L1_ffn_ln1_g': _L1_ffn_in['ln1_g'], 'L1_ffn_ln1_b': _L1_ffn_in['ln1_b'], 'L1_ffn_Wqkv': _L1_ffn_in['Wqkv'], 'L1_ffn_Wproj': _L1_ffn_in['Wproj'], 'L1_ffn_ln2_g': _L1_ffn_in['ln2_g'], 'L1_ffn_ln2_b': _L1_ffn_in['ln2_b'], 'L1_ffn_Wgate': _L1_ffn_in['Wgate'], 'L1_ffn_W1': _L1_ffn_in['W1'], 'L1_ffn_b1': _L1_ffn_in['b1'], 'L1_ffn_W2': _L1_ffn_in['W2'], 'L1_ffn_b2': _L1_ffn_in['b2']}
    _x0 = _d['L0_attn_x']
    _d['L0_attn_x'] = jax.random.normal(jax.random.fold_in(jax.random.key(seed), 1), (8, 1024, 256), dtype=_x0.dtype)
    del _x0
    return _d

def reference(L0_attn_x, L0_attn_Wq, L0_attn_Wk, L0_attn_Wv, L0_attn_Wo, L0_ffn_w_up, L0_ffn_w_down, L1_attn_time_maa_x, L1_attn_time_maa_rg, L1_attn_time_maa_wa, L1_attn_time_maa_k, L1_attn_time_maa_v, L1_attn_time_maa_w1, L1_attn_time_maa_w2, L1_attn_time_decay, L1_attn_time_decay_w1, L1_attn_time_decay_w2, L1_attn_time_faaaa, L1_attn_time_aaaaa, L1_attn_time_aaa_w1, L1_attn_time_aaa_w2, L1_attn_time_kkk_w1, L1_attn_time_kkk_w2, L1_attn_gate_w1, L1_attn_gate_w2, L1_attn_ma_w1, L1_attn_ma_w2, L1_attn_time_misc_a, L1_attn_mk_w1, L1_attn_mk_w2, L1_attn_time_misc_k, L1_attn_w_receptance, L1_attn_w_key, L1_attn_w_value, L1_attn_w_output, L1_attn_ln_w, L1_attn_ln_b, L1_ffn_ln1_g, L1_ffn_ln1_b, L1_ffn_Wqkv, L1_ffn_Wproj, L1_ffn_ln2_g, L1_ffn_ln2_b, L1_ffn_Wgate, L1_ffn_W1, L1_ffn_b1, L1_ffn_W2, L1_ffn_b2):

    def _L0_attn_ref(x, Wq, Wk, Wv, Wo):
        import jax, jax.numpy as jnp
        import numpy as np
        B, S, D, K = (4, 1024, 256, 64)
        Q = jax.nn.elu(x @ Wq.T) + 1.0
        Kf = jax.nn.elu(x @ Wk.T) + 1.0
        V = x @ Wv.T
        KV_sum = jnp.cumsum(Kf[..., :, None] * V[..., None, :], axis=1)
        K_sum = jnp.cumsum(Kf, axis=1)
        num = jnp.einsum('bsk,bskm->bsm', Q, KV_sum)
        den = jnp.einsum('bsk,bsk->bs', Q, K_sum)[..., None]
        out = num / (den + 1e-06)
        return out @ Wo.T

    def _L0_ffn_ref(x, w_up, w_down):
        import jax, jax.numpy as jnp
        import numpy as np
        EPS = 1e-08

        def _ternary_linear(x, w):
            alpha = jnp.mean(jnp.abs(w))
            w_t = jnp.sign(w) * (jnp.abs(w) > 0.5 * alpha).astype(w.dtype)
            w_q = w + jax.lax.stop_gradient(w_t - w)
            d = x.shape[-1]
            rms = jnp.sqrt(jnp.sum(x * x, axis=-1, keepdims=True)) / jnp.sqrt(jnp.asarray(d, x.dtype))
            x_norm = x / (rms + EPS)
            return jnp.einsum('bsd,fd->bsf', x_norm, w_q)
        h = jax.nn.gelu(_ternary_linear(x, w_up), approximate=False)
        return _ternary_linear(h, w_down)

    def _L1_attn_ref(x, time_maa_x, time_maa_rg, time_maa_wa, time_maa_k, time_maa_v, time_maa_w1, time_maa_w2, time_decay, time_decay_w1, time_decay_w2, time_faaaa, time_aaaaa, time_aaa_w1, time_aaa_w2, time_kkk_w1, time_kkk_w2, gate_w1, gate_w2, ma_w1, ma_w2, time_misc_a, mk_w1, mk_w2, time_misc_k, w_receptance, w_key, w_value, w_output, ln_w, ln_b):
        import jax, jax.numpy as jnp
        import numpy as np
        from jax import lax
        B, T, C = (4, 256, 256)
        N = 64
        H = C // N
        D_MIX, D_DECAY, D_LORA, D_GATE = (32, 64, 16, 128)
        EPS = 0.00064

        def wkv7(r, w, k, v, a, b):
            B_, T_, C_ = r.shape
            resh = lambda t: t.reshape(B_, T_, H, N).transpose(1, 0, 2, 3)
            rT, kT, vT, aT, bT = map(resh, (r, k, v, a, b))
            dT = jnp.exp(resh(w))

            def step(S, inp):
                rt, dt, kt, vt, at, bt = inp
                sa = jnp.einsum('bhij,bhj->bhi', S, at)
                S = S * dt[:, :, None, :] + sa[..., None] * bt[:, :, None, :] + vt[..., None] * kt[:, :, None, :]
                y = jnp.einsum('bhij,bhj->bhi', S, rt)
                return (S, y)
            S0 = jnp.zeros((B_, H, N, N), r.dtype)
            _, ys = lax.scan(step, S0, (rT, dT, kT, vT, aT, bT))
            return ys.transpose(1, 0, 2, 3).reshape(B_, T_, C_)

        def _forward(x, time_maa_x, time_maa_rg, time_maa_wa, time_maa_k, time_maa_v, time_maa_w1, time_maa_w2, time_decay, time_decay_w1, time_decay_w2, time_faaaa, time_aaaaa, time_aaa_w1, time_aaa_w2, time_kkk_w1, time_kkk_w2, gate_w1, gate_w2, ma_w1, ma_w2, time_misc_a, mk_w1, mk_w2, time_misc_k, w_receptance, w_key, w_value, w_output, ln_w, ln_b):
            B_, T_, C_ = x.shape
            xprev = jnp.concatenate([jnp.zeros_like(x[:, :1]), x[:, :-1]], axis=1)
            xx = xprev - x
            mix_in = jnp.tanh((x + xx * time_maa_x) @ time_maa_w1)
            mix = jnp.einsum('btfd,fdc->fbtc', mix_in.reshape(B_, T_, 4, D_MIX), time_maa_w2)
            mrg, mwa, mk_, mv_ = (mix[0], mix[1], mix[2], mix[3])
            xrg = x + xx * (time_maa_rg + mrg)
            xwa = x + xx * (time_maa_wa + mwa)
            xk = x + xx * (time_maa_k + mk_)
            xv = x + xx * (time_maa_v + mv_)
            r = xrg @ w_receptance.T
            w = -jax.nn.softplus(-(time_decay + jnp.tanh(xwa @ time_decay_w1) @ time_decay_w2)) - 0.5
            k = xk @ w_key.T
            v = xv @ w_value.T
            g = jnp.tanh(xrg @ gate_w1) @ gate_w2
            kk = k + jnp.tanh(xk @ time_kkk_w1) @ time_kkk_w2
            kk4 = kk.reshape(B_, T_, H, N)
            kk4 = kk4 / jnp.maximum(jnp.linalg.norm(kk4, axis=-1, keepdims=True), 1e-12)
            kk = kk4.reshape(B_, T_, C_)
            a = jax.nn.sigmoid(time_aaaaa + xwa @ time_aaa_w1 @ time_aaa_w2)
            ma = jax.nn.sigmoid(time_misc_a + xwa @ ma_w1 @ ma_w2)
            k = k * ma + k * a * (1.0 - ma)
            mk2 = jax.nn.sigmoid(time_misc_k + xk @ mk_w1 @ mk_w2)
            k = k * jnp.exp(jnp.minimum(w * mk2, 0.0))
            y = wkv7(r, w, k, v, -kk, kk * a)
            yh = y.reshape(B_ * T_, H, N)
            mu = yh.mean(-1, keepdims=True)
            var = yh.var(-1, keepdims=True)
            yh = (yh - mu) * lax.rsqrt(var + EPS)
            y = (yh.reshape(B_ * T_, C_) * ln_w + ln_b).reshape(B_, T_, C_)
            rr = r.reshape(B_, T_, H, N)
            kr = k.reshape(B_, T_, H, N)
            vr = v.reshape(B_, T_, H, N)
            y = y + ((rr * kr * time_faaaa).sum(-1, keepdims=True) * vr).reshape(B_, T_, C_)
            return y * g @ w_output.T
        return _forward(x, time_maa_x, time_maa_rg, time_maa_wa, time_maa_k, time_maa_v, time_maa_w1, time_maa_w2, time_decay, time_decay_w1, time_decay_w2, time_faaaa, time_aaaaa, time_aaa_w1, time_aaa_w2, time_kkk_w1, time_kkk_w2, gate_w1, gate_w2, ma_w1, ma_w2, time_misc_a, mk_w1, mk_w2, time_misc_k, w_receptance, w_key, w_value, w_output, ln_w, ln_b)

    def _L1_ffn_ref(x, ln1_g, ln1_b, Wqkv, Wproj, ln2_g, ln2_b, Wgate, W1, b1, W2, b2):
        import jax, jax.numpy as jnp
        import numpy as np
        import math
        B, T, D, H, E, TOPK, CAPF = (4, 512, 256, 16, 8, 2, 2.0)
        HD = D // H

        def layernorm(x, g, b, eps=1e-05):
            m = jnp.mean(x, -1, keepdims=True)
            v = jnp.mean(jnp.square(x - m), -1, keepdims=True)
            return (x - m) * jax.lax.rsqrt(v + eps) * g + b

        def block_forward(x, ln1_g, ln1_b, Wqkv, Wproj, ln2_g, ln2_b, Wgate, W1, b1, W2, b2):
            Bb, Tt, d = x.shape
            hd = HD
            half = hd // 2
            h = layernorm(x, ln1_g, ln1_b)
            qkv = (h @ Wqkv).reshape(Bb, Tt, H, 3 * hd)
            q, k, v = (qkv[..., :hd], qkv[..., hd:2 * hd], qkv[..., 2 * hd:])
            inv_freq = 1.0 / 10000.0 ** (jnp.arange(0, hd, 2, dtype=jnp.float32) / hd)
            ang = jnp.arange(Tt, dtype=jnp.float32)[:, None] * inv_freq
            sin = jnp.sin(ang)[None, :, None, :].astype(x.dtype)
            cos = jnp.cos(ang)[None, :, None, :].astype(x.dtype)

            def rope(t):
                t1, t2 = (t[..., :half], t[..., half:])
                return jnp.concatenate([t1 * cos - t2 * sin, t1 * sin + t2 * cos], -1)
            q, k = (rope(q), rope(k))
            scores = jnp.einsum('bqhd,bkhd->bhqk', q, k) / math.sqrt(hd)
            causal = jnp.tril(jnp.ones((Tt, Tt), dtype=bool))
            scores = jnp.where(causal, scores, jnp.asarray(-1000000000.0, scores.dtype))
            probs = jax.nn.softmax(scores, axis=-1)
            attn = jnp.einsum('bhqk,bkhd->bqhd', probs, v).reshape(Bb, Tt, d) @ Wproj
            x = x + attn
            h2 = layernorm(x, ln2_g, ln2_b)
            flat = h2.reshape(-1, d)
            N = flat.shape[0]
            capacity = int(math.ceil(CAPF * N / E))
            gates = jax.nn.softmax((flat @ Wgate).astype(jnp.float32), -1).astype(flat.dtype)
            _, top_inds = jax.lax.top_k(gates, TOPK)
            mask = jnp.zeros((N, E), dtype=bool).at[jnp.arange(N)[:, None], top_inds].set(True)
            pos = jnp.cumsum(mask.astype(jnp.int32), axis=0) * mask - 1
            keep = (pos < capacity) & mask
            t_flat = jnp.repeat(jnp.arange(N), TOPK)
            e_flat = top_inds.reshape(-1)
            p = pos[t_flat, e_flat]
            kp = keep[t_flat, e_flat]
            p_eff = jnp.where(kp, p, capacity)
            exp_in = jnp.zeros((E, capacity, d), flat.dtype).at[e_flat, p_eff].set(flat[t_flat], mode='drop')
            hmid = jax.nn.gelu(jnp.einsum('ecd,edf->ecf', exp_in, W1) + b1[:, None, :], approximate=False)
            exp_out = jnp.einsum('ecf,efd->ecd', hmid, W2) + b2[:, None, :]
            gate = gates[t_flat, e_flat] * kp.astype(flat.dtype)
            p_g = jnp.minimum(p_eff, capacity - 1)
            moe = jnp.zeros((N, d), flat.dtype).at[t_flat].add(exp_out[e_flat, p_g] * gate[:, None])
            return x + moe.reshape(Bb, Tt, d)
        return block_forward(x, ln1_g, ln1_b, Wqkv, Wproj, ln2_g, ln2_b, Wgate, W1, b1, W2, b2)
    x = L0_attn_x
    xn = _layernorm(x, axis=-1)
    x = x + _L0_attn_ref(xn, L0_attn_Wq, L0_attn_Wk, L0_attn_Wv, L0_attn_Wo) + _L0_ffn_ref(xn, L0_ffn_w_up, L0_ffn_w_down)
    xn = _layernorm(x, axis=-1)
    x = x + _L1_attn_ref(xn, L1_attn_time_maa_x, L1_attn_time_maa_rg, L1_attn_time_maa_wa, L1_attn_time_maa_k, L1_attn_time_maa_v, L1_attn_time_maa_w1, L1_attn_time_maa_w2, L1_attn_time_decay, L1_attn_time_decay_w1, L1_attn_time_decay_w2, L1_attn_time_faaaa, L1_attn_time_aaaaa, L1_attn_time_aaa_w1, L1_attn_time_aaa_w2, L1_attn_time_kkk_w1, L1_attn_time_kkk_w2, L1_attn_gate_w1, L1_attn_gate_w2, L1_attn_ma_w1, L1_attn_ma_w2, L1_attn_time_misc_a, L1_attn_mk_w1, L1_attn_mk_w2, L1_attn_time_misc_k, L1_attn_w_receptance, L1_attn_w_key, L1_attn_w_value, L1_attn_w_output, L1_attn_ln_w, L1_attn_ln_b) + _L1_ffn_ref(xn, L1_ffn_ln1_g, L1_ffn_ln1_b, L1_ffn_Wqkv, L1_ffn_Wproj, L1_ffn_ln2_g, L1_ffn_ln2_b, L1_ffn_Wgate, L1_ffn_W1, L1_ffn_b1, L1_ffn_W2, L1_ffn_b2)
    return x

_drawn_inputs = setup_inputs


def setup_inputs(seed=0):
    import zlib

    import numpy as np

    out = dict(_drawn_inputs(seed))
    spreads = {'L1_attn_time_aaaaa': (0.0, 0.8),
     'L1_attn_time_misc_a': (0.0, 0.8),
     'L1_attn_time_misc_k': (0.0, 0.8),
     'L1_attn_ln_w': (1.0, 0.6),
     'L1_attn_ln_b': (0.0, 2.0),
     'L1_ffn_ln1_g': (1.0, 0.6),
     'L1_ffn_ln1_b': (0.0, 2.0),
     'L1_ffn_ln2_g': (1.0, 0.6),
     'L1_ffn_ln2_b': (0.0, 2.0),
     'L1_ffn_b1': (0.0, 2.0),
     'L1_ffn_b2': (0.0, 2.0)}
    factors = {'L0_attn_Wq': 8.0,
     'L0_attn_Wk': 8.0,
     'L0_attn_Wv': 8.0,
     'L0_attn_Wo': 8.0,
     'L1_attn_time_maa_x': 8.0,
     'L1_attn_time_maa_rg': 8.0,
     'L1_attn_time_maa_wa': 8.0,
     'L1_attn_time_maa_k': 8.0,
     'L1_attn_time_maa_v': 8.0,
     'L1_attn_time_maa_w1': 8.0,
     'L1_attn_time_maa_w2': 8.0,
     'L1_attn_time_decay': 8.0,
     'L1_attn_time_decay_w1': 8.0,
     'L1_attn_time_decay_w2': 8.0,
     'L1_attn_time_faaaa': 8.0,
     'L1_attn_time_aaa_w1': 8.0,
     'L1_attn_time_aaa_w2': 8.0,
     'L1_attn_time_kkk_w1': 64.0,
     'L1_attn_time_kkk_w2': 64.0,
     'L1_attn_gate_w1': 8.0,
     'L1_attn_gate_w2': 8.0,
     'L1_attn_ma_w1': 8.0,
     'L1_attn_ma_w2': 8.0,
     'L1_attn_mk_w1': 8.0,
     'L1_attn_mk_w2': 8.0,
     'L1_attn_w_receptance': 8.0,
     'L1_attn_w_key': 8.0,
     'L1_attn_w_value': 8.0,
     'L1_attn_w_output': 8.0,
     'L1_ffn_Wqkv': 64.0,
     'L1_ffn_Wproj': 64.0,
     'L1_ffn_Wgate': 64.0,
     'L1_ffn_W1': 64.0,
     'L1_ffn_W2': 64.0}
    for name, (base, spread) in spreads.items():
        noise = np.random.default_rng([zlib.crc32(name.encode()), seed]).standard_normal(out[name].shape)
        drawn = base * np.exp(spread * noise) if base else spread * noise
        out[name] = jnp.asarray(drawn.astype(out[name].dtype))
    for name, factor in factors.items():
        out[name] = (out[name] * factor).astype(out[name].dtype)
    return out
```

```python
from contextlib import ExitStack, contextmanager

import numpy as np

import concourse.bass as bass
from concourse import mybir

F32 = mybir.dt.float32
BF16 = mybir.dt.bfloat16
U32 = mybir.dt.uint32
ALU = mybir.AluOpType
ACT = mybir.ActivationFunctionType
AX = mybir.AxisListType

P = 128
B, S, D = 8, 1024, 256
N = B * S
DC = D // P
G = 4
GT = G * P
LK = 64
FF = 1024
FC = FF // P
HEADS = 4
HN = 64
CH = 32
QN = P // CH
AH, AD = 16, 16
E = 8
CAP = 2 * N // E
NSEM = 60


class Signals:

    def __init__(self, pool):
        self.pool, self.names = pool, {}

    def __call__(self, name):
        if name not in self.names:
            self.names[name] = len(self.names)
        return self.pool[self.names[name]]


class Program:
    def __init__(self, nc, ctx):
        self.nc = nc
        self.pool = [ctx.enter_context(nc.semaphore(f"signal{i}")) for i in range(NSEM)]
        first = self.pool[0].num
        assert [s.num for s in self.pool] == list(range(first, first + NSEM))
        self.span = range(first, first + NSEM)

    @contextmanager
    def body(self):
        signals = Signals(self.pool)
        with self.nc.Block() as block:
            yield block, signals
        with self.nc.Block() as block:
            @block.gpsimd
            def _(pool):
                pool.sem_clear(self.span)


def rows(t, n, count):
    return t[bass.ds(n * count, count), :].rearrange("(u p) c -> p u c", p=P)


def wide(ap, n):
    return ap.unsqueeze(1).to_broadcast([ap.shape[0], n, ap.shape[1]])


def constants(pr, sb, io):
    nc = pr.nc
    c = {}
    c["ident"] = sb("ident", [P, P])
    c["ones"] = sb("ones", [P, P])
    c["upper"] = sb("upper", [P, P])
    c["half"] = sb("half", [P, G])
    c["minus_half"] = sb("minus_half", [P, G * HEADS])
    with pr.body() as (block, s):
        @block.gpsimd
        def _(pool):
            pool.memset(c["half"][:, :], 0.5)
            pool.memset(c["minus_half"][:, :], -0.5)
            pool.memset(c["ident"][:, :], 0.0).then_inc(s("filled"), 1)
            pool.memset(c["ones"][:, :], 1.0).then_inc(s("filled"), 1)
            pool.wait_ge(s("filled"), 2)
            pool.affine_select(out=c["ident"][:, :], in_=c["ident"][:, :], compare_op=ALU.not_equal, fill=1.0,
                               base=0, pattern=[[-1, P]], channel_multiplier=1)
            pool.affine_select(out=c["upper"][:, :], in_=c["ones"][:, :], compare_op=ALU.is_ge, fill=0.0,
                               base=0, pattern=[[1, P]], channel_multiplier=-1)
    return c


def layer0_attention(pr, io, c):
    nc = pr.nc
    with ExitStack() as ctx:
        def sb(name, shape):
            return ctx.enter_context(nc.sbuf_tensor("a_" + name, shape, F32))

        ps = [ctx.enter_context(nc.psum_tensor(f"a_bank{i}", [P, 512], F32)) for i in range(8)]
        wq, wk = sb("wq", [P, DC, LK]), sb("wk", [P, DC, LK])
        wkv = sb("wkv", [P, DC, 2 * LK])
        wo = sb("wo", [LK, D])
        x = sb("x", [P, G, D])
        stats, mv = sb("stats", [P, G, 6]), sb("mv", [P, G, 2])
        var = sb("var", [P, G])
        rstd, ms, rms, scale = sb("rstd", [P, G]), sb("ms", [P, G]), sb("rms", [P, G]), sb("scale", [P, G])
        xn, xs = sb("xn", [P, G, D]), sb("xs", [P, G, D])
        xnt = sb("xnt", [P, DC, GT])
        low, qft, kft = sb("low", [LK, 2, GT]), sb("qft", [LK, GT]), sb("kft", [LK, GT])
        lowk, kf = sb("lowk", [P, G, LK]), sb("kf", [P, G, LK])
        va = sb("va", [P, G, LK + 1])
        sc = sb("sc", [P, GT])
        state = sb("state", [LK, G + 1, LK + 1])
        den = sb("den", [P, G, 1])
        ao, aot = sb("ao", [P, G, LK]), sb("aot", [LK, GT])
        a = sb("a", [P, G, D])
        with pr.body() as (block, s):
            @block.sync
            def _(sp):
                sp.dma_start(wq[:, :, :], io["L0_attn_Wq_T"].rearrange("(c p) n -> p c n", p=P)).then_inc(s("w"), 16)
                sp.dma_start(wk[:, :, :], io["L0_attn_Wk_T"].rearrange("(c p) n -> p c n", p=P)).then_inc(s("w"), 16)
                sp.dma_start(wkv[:, :, 0:LK], io["L0_attn_Wk_T"].rearrange("(c p) n -> p c n", p=P)).then_inc(s("w"), 16)
                sp.dma_start(wkv[:, :, LK:2 * LK], io["L0_attn_Wv_T"].rearrange("(c p) n -> p c n", p=P)).then_inc(s("w"), 16)
                sp.dma_start(wo[:, :], io["L0_attn_Wo_T"]).then_inc(s("w"), 16)
                sp.wait_ge(s("w"), 80)

            @block.vector
            def _(dve):
                dve.memset(va[:, :, :], 1.0)

        with nc.Fori(0, B) as b:
            with pr.body() as (block, s):
                @block.vector
                def _(dve):
                    dve.memset(state[:, 0, :], 0.0)
            with nc.Fori(0, S // GT) as g:
                n = b * (S // GT) + g
                with pr.body() as (block, s):
                    @block.sync
                    def _(sp):
                        sp.dma_start(x[:, :, :], rows(io["L0_attn_x"], n, GT)).then_inc(s("x_here"), 16)
                        sp.wait_ge(s("xs_ready"), G)
                        sp.dma_start(rows(io["s_xs"], n, GT), xs[:, :, :]).then_inc(s("stored"), 16)
                        sp.wait_ge(s("a_ready"), G // 2)
                        sp.dma_start(rows(io["s_a"], n, GT), a[:, :, :]).then_inc(s("stored"), 16)
                        sp.wait_ge(s("stored"), 32)

                    @block.gpsimd
                    def _(pool):
                        pool.wait_ge(s("var_ready"), 1)
                        pool.tensor_tensor(rstd[:, :], var[:, :], c["minus_half"][:, 0:G], ALU.pow).then_inc(s("rstd_ready"), 1)
                        pool.wait_ge(s("ms_ready"), 1)
                        pool.tensor_tensor(rms[:, :], ms[:, :], c["half"][:, :], ALU.pow).then_inc(s("rms_ready"), 1)

                    @block.scalar
                    def _(act):
                        for k in range(DC):
                            act.wait_ge(s("xnt_turned"), 4 * (k + 1))
                            act.activation(xnt[:, k, :], ps[k][:, :], ACT.Copy).then_inc(s("xnt_ready"), 1)
                        for k in range(2):
                            act.wait_ge(s("low_ready"), k + 1)
                            act.activation(low[:, k, :], low[:, k, :], ACT.Exp).then_inc(s("exp_ready"), 1)
                        act.wait_ge(s("lowk_ready"), 1)
                        act.activation(lowk[:, :, :], lowk[:, :, :], ACT.Exp).then_inc(s("exp_ready"), 1)
                        act.wait_ge(s("ao_turned"), G)
                        act.activation(aot[:, :], ps[1][0:LK, :], ACT.Copy).then_inc(s("aot_ready"), 1)

                    @block.tensor
                    def _(pe):
                        for k in range(DC):
                            for u in range(G):
                                if k == 0:
                                    pe.wait_ge(s("xn_ready"), u + 1)
                                pe.transpose(ps[k][:, u * P:(u + 1) * P], xn[:, u, k * P:(k + 1) * P],
                                             c["ident"][:, :]).then_inc(s("xnt_turned"), 1)
                        pe.wait_ge(s("xnt_ready"), DC)
                        for j, w in enumerate((wq, wk)):
                            for k in range(DC):
                                mm = pe.matmul(ps[2 + j][0:LK, :], w[:, k, :], xnt[:, k, :], start=k == 0, stop=k == DC - 1)
                            mm.then_inc(s("qk_made"), 1)
                        for u in range(G):
                            for k in range(DC):
                                mm = pe.matmul(ps[4][:, u * P:(u + 1) * P], xnt[:, k, u * P:(u + 1) * P], wkv[:, k, :],
                                               start=k == 0, stop=k == DC - 1)
                        mm.then_inc(s("kv_made"), 1)
                        pe.wait_ge(s("qft_ready"), 1)
                        pe.wait_ge(s("kft_ready"), 1)
                        for u in range(G):
                            mm = pe.matmul(ps[5][:, u * P:(u + 1) * P], kft[:, u * P:(u + 1) * P], qft[:, u * P:(u + 1) * P],
                                           start=True, stop=True)
                        mm.then_inc(s("sc_made"), 1)
                        pe.wait_ge(s("kf_ready"), 1)
                        pe.wait_ge(s("va_ready"), 1)
                        for u in range(G):
                            mm = pe.matmul(ps[6][0:LK, u * (LK + 1):(u + 1) * (LK + 1)], kf[:, u, :], va[:, u, :],
                                           start=True, stop=True)
                        mm.then_inc(s("ds_made"), 1)
                        pe.wait_ge(s("sc_ready"), 1)
                        for u in range(G):
                            pe.wait_ge(s("state_ready"), u + 1)
                            out = ps[7][:, u * (LK + 1):(u + 1) * (LK + 1)]
                            pe.matmul(out, sc[:, u * P:(u + 1) * P], va[:, u, :], start=True, stop=False)
                            mm = pe.matmul(out, qft[:, u * P:(u + 1) * P], state[:, u, :], start=False, stop=True)
                        mm.then_inc(s("num_made"), 1)
                        pe.wait_ge(s("ao_ready"), 1)
                        for u in range(G):
                            pe.transpose(ps[1][0:LK, u * P:(u + 1) * P], ao[:, u, :], c["ident"][:, :]).then_inc(s("ao_turned"), 1)
                        pe.wait_ge(s("aot_ready"), 1)
                        for u in range(G):
                            mm = pe.matmul(ps[2 + u // 2][:, (u % 2) * D:(u % 2 + 1) * D], aot[:, u * P:(u + 1) * P], wo[:, :],
                                           start=True, stop=True)
                            if u % 2:
                                mm.then_inc(s("y_made"), 1)

                    @block.vector
                    def _(dve):
                        dve.wait_ge(s("x_here"), 16)
                        for u in range(G):
                            dve.bn_stats(stats[:, u, :], x[:, u, :]).then_inc(s("stats_ready"), 1)
                        for u in range(G):
                            dve.wait_ge(s("stats_ready"), u + 1)
                            dve.bn_aggr(mv[:, u, :], stats[:, u, :]).then_inc(s("mv_ready"), 1)
                        dve.wait_ge(s("mv_ready"), G)
                        dve.tensor_scalar(var[:, :], mv[:, :, 1], 1e-5, None, ALU.add).then_inc(s("var_ready"), 1)
                        dve.wait_ge(s("rstd_ready"), 1)
                        for u in range(G):
                            dve.tensor_scalar(xn[:, u, :], x[:, u, :], mv[:, u, 0:1], rstd[:, u:u + 1], ALU.subtract,
                                              ALU.mult).then_inc(s("xn_ready"), 1)
                        dve.tensor_tensor(ms[:, :], rstd[:, :], rstd[:, :], ALU.mult).then_inc(s("rstd2_ready"), 1)
                        dve.wait_ge(s("rstd2_ready"), 1)
                        dve.tensor_tensor(ms[:, :], ms[:, :], mv[:, :, 1], ALU.mult).then_inc(s("ms_ready"), 1)
                        dve.wait_ge(s("rms_ready"), 1)
                        dve.tensor_scalar(scale[:, :], rms[:, :], 1e-8, None, ALU.add).then_inc(s("scale_ready"), 1)
                        dve.wait_ge(s("scale_ready"), 1)
                        dve.reciprocal(scale[:, :], scale[:, :]).then_inc(s("scale_ready"), 1)
                        dve.wait_ge(s("scale_ready"), 2)
                        dve.wait_ge(s("xn_ready"), G)
                        for u in range(G):
                            dve.tensor_scalar(xs[:, u, :], xn[:, u, :], scale[:, u:u + 1], None, ALU.mult).then_inc(s("xs_ready"), 1)
                        for k in range(2):
                            dve.wait_ge(s("qk_made"), k + 1)
                            dve.tensor_scalar(low[:, k, :], ps[2 + k][0:LK, :], 0.0, None, ALU.min).then_inc(s("low_ready"), 1)
                        kraw = ps[4][:, :].rearrange("p (g n) -> p g n", g=G)[:, :, 0:LK]
                        dve.wait_ge(s("kv_made"), 1)
                        dve.tensor_scalar(lowk[:, :, :], kraw, 0.0, None, ALU.min).then_inc(s("lowk_ready"), 1)
                        dve.tensor_copy(va[:, :, 0:LK], ps[4][:, :].rearrange("p (g n) -> p g n", g=G)[:, :, LK:2 * LK]
                                        ).then_inc(s("va_ready"), 1)
                        for k, (out, name) in enumerate(((qft, "qft_ready"), (kft, "kft_ready"))):
                            dve.wait_ge(s("exp_ready"), k + 1)
                            dve.scalar_tensor_tensor(out[:, :], ps[2 + k][0:LK, :], 0.0, low[:, k, :], ALU.max,
                                                     ALU.add).then_inc(s(name), 1)
                        dve.wait_ge(s("exp_ready"), 3)
                        dve.scalar_tensor_tensor(kf[:, :, :], kraw, 0.0, lowk[:, :, :], ALU.max, ALU.add).then_inc(s("kf_ready"), 1)
                        dve.wait_ge(s("sc_made"), 1)
                        dve.tensor_tensor(sc[:, :].rearrange("p (g n) -> p g n", g=G),
                                          ps[5][:, :].rearrange("p (g n) -> p g n", g=G), wide(c["upper"][:, :], G),
                                          ALU.mult).then_inc(s("sc_ready"), 1)
                        dve.wait_ge(s("ds_made"), 1)
                        dve.engine_nop().then_inc(s("state_ready"), 1)
                        for u in range(G):
                            dve.wait_ge(s("state_ready"), u + 1)
                            dve.tensor_tensor(state[:, u + 1, :], state[:, u, :], ps[6][0:LK, u * (LK + 1):(u + 1) * (LK + 1)],
                                              ALU.add).then_inc(s("state_ready"), 1)
                        num = ps[7][:, 0:G * (LK + 1)].rearrange("p (g n) -> p g n", g=G)
                        dve.wait_ge(s("num_made"), 1)
                        dve.tensor_scalar(den[:, :, :], num[:, :, LK:LK + 1], 1e-6, None, ALU.add).then_inc(s("den_ready"), 1)
                        dve.wait_ge(s("den_ready"), 1)
                        dve.reciprocal(den[:, :, :], den[:, :, :]).then_inc(s("den_ready"), 1)
                        dve.wait_ge(s("den_ready"), 2)
                        dve.tensor_tensor(ao[:, :, :], num[:, :, 0:LK], den[:, :, :].to_broadcast([P, G, LK]),
                                          ALU.mult).then_inc(s("ao_ready"), 1)
                        dve.wait_ge(s("state_ready"), G + 1)
                        dve.tensor_copy(state[:, 0, :], state[:, G, :])
                        for h in range(2):
                            dve.wait_ge(s("y_made"), h + 1)
                            dve.tensor_tensor(a[:, 2 * h:2 * h + 2, :], ps[2 + h][:, :].rearrange("p (g n) -> p g n", g=2),
                                              x[:, 2 * h:2 * h + 2, :], ALU.add).then_inc(s("a_ready"), 1)


def feed_forward(pe, act, s, ps, xt, w1, w2, ht, bias, stage):
    if stage == "pe":
        for k in range(DC):
            pe.wait_ge(s("xt_ready"), k + 1)
        for f in range(FC):
            if f >= 4:
                pe.wait_ge(s("ht_ready"), f - 3)
            for k in range(DC):
                mm = pe.matmul(ps[f % 4][:, :], w1[:, k, f * P:(f + 1) * P], xt[:, k, :], start=k == 0, stop=k == DC - 1)
            mm.then_inc(s("h_made"), 1)
        for u in range(G):
            for f in range(FC):
                if u == 0:
                    pe.wait_ge(s("ht_ready"), f + 1)
                mm = pe.matmul(ps[4 + u // 2][:, (u % 2) * D:(u % 2 + 1) * D], ht[:, f, u * P:(u + 1) * P], w2[:, f, :],
                               start=f == 0, stop=f == FC - 1)
            if u % 2:
                mm.then_inc(s("y_made"), 1)
    else:
        for f in range(FC):
            act.wait_ge(s("h_made"), f + 1)
            if bias is None:
                act.activation(ht[:, f, :], ps[f % 4][:, :], ACT.Gelu).then_inc(s("ht_ready"), 1)
            else:
                act.activation(ht[:, f, :], ps[f % 4][:, :], ACT.Gelu, bias=bias[:, f:f + 1]).then_inc(s("ht_ready"), 1)


def layer0_feed_forward(pr, io, c):
    nc = pr.nc
    with ExitStack() as ctx:
        def sb(name, shape):
            return ctx.enter_context(nc.sbuf_tensor("f_" + name, shape, F32))

        ps = [ctx.enter_context(nc.psum_tensor(f"f_bank{i}", [P, 512], F32)) for i in range(8)]
        w1, w2 = sb("w1", [P, DC, FF]), sb("w2", [P, FC, D])
        below = sb("below", [P, DC * FF])
        total, limit, minus = sb("total", [P, 2]), sb("limit", [P, 2]), sb("minus", [P, 2])
        xs, a = sb("xs", [P, G, D]), sb("a", [P, G, D])
        xt, ht = sb("xt", [P, DC, GT]), sb("ht", [P, FC, GT])
        sq, sum_sq = sb("sq", [P, FC, GT]), sb("sum_sq", [P, GT])
        ms, rms = sb("ms", [P, G]), sb("rms", [P, G])
        x1, xn = sb("x1", [P, G, D]), sb("xn", [P, G, D])
        stats, mv, var, rstd = sb("stats", [P, G, 6]), sb("mv", [P, G, 2]), sb("var", [P, G]), sb("rstd", [P, G])
        flat = [w1[:, :, :].rearrange("p c n -> p (c n)"), w2[:, :, :].rearrange("p c n -> p (c n)")]
        with pr.body() as (block, s):
            @block.sync
            def _(sp):
                sp.dma_start(w1[:, :, :], io["L0_ffn_w_up_T"].rearrange("(c p) n -> p c n", p=P)).then_inc(s("w_here"), 16)
                sp.dma_start(w2[:, :, :], io["L0_ffn_w_down_T"].rearrange("(c p) n -> p c n", p=P)).then_inc(s("w_here"), 16)

            @block.tensor
            def _(pe):
                pe.wait_ge(s("total_ready"), 2)
                pe.matmul(ps[0][:, 0:2], c["ones"][:, :], total[:, :], start=True, stop=True).then_inc(s("sum_made"), 1)

            @block.vector
            def _(dve):
                dve.wait_ge(s("w_here"), 32)
                for j in range(2):
                    dve.tensor_reduce(total[:, j:j + 1], flat[j], AX.X, ALU.add, apply_absolute_value=True).then_inc(s("total_ready"), 1)
                dve.wait_ge(s("sum_made"), 1)
                dve.tensor_scalar(limit[:, :], ps[0][:, 0:2], 0.5 / (D * FF), None, ALU.mult).then_inc(s("limit_ready"), 1)
                dve.tensor_scalar(minus[:, :], ps[0][:, 0:2], -0.5 / (D * FF), None, ALU.mult).then_inc(s("limit_ready"), 1)
                dve.wait_ge(s("limit_ready"), 2)
                for j in range(2):
                    dve.tensor_scalar(below[:, :], flat[j], minus[:, j:j + 1], None, ALU.is_lt).then_inc(s("below_ready"), 1)
                    dve.wait_ge(s("below_ready"), 2 * j + 1)
                    dve.scalar_tensor_tensor(flat[j], flat[j], limit[:, j:j + 1], below[:, :], ALU.is_gt,
                                             ALU.subtract).then_inc(s("below_ready"), 1)
                    dve.wait_ge(s("below_ready"), 2 * j + 2)

        with nc.Fori(0, N // GT) as n:
            with pr.body() as (block, s):
                @block.sync
                def _(sp):
                    sp.dma_start(xs[:, :, :], rows(io["s_xs"], n, GT)).then_inc(s("xs_here"), 16)
                    sp.dma_start(a[:, :, :], rows(io["s_a"], n, GT)).then_inc(s("a_here"), 16)
                    sp.wait_ge(s("x1_ready"), G)
                    sp.dma_start(rows(io["s_x1"], n, GT), x1[:, :, :]).then_inc(s("stored"), 16)
                    sp.wait_ge(s("xn_ready"), G)
                    sp.dma_start(rows(io["s_xn"], n, GT), xn[:, :, :]).then_inc(s("stored"), 16)
                    sp.wait_ge(s("stored"), 32)

                @block.gpsimd
                def _(pool):
                    for f in range(FC // 2, FC):
                        pool.wait_ge(s("ht_ready"), f + 1)
                        pool.tensor_tensor(sq[:, f, :], ht[:, f, :], ht[:, f, :], ALU.mult).then_inc(s("sq_ready_b"), 1)
                    pool.wait_ge(s("ms_ready"), 1)
                    pool.tensor_tensor(rms[:, :], ms[:, :], c["half"][:, :], ALU.pow).then_inc(s("rms_ready"), 1)
                    pool.wait_ge(s("var_ready"), 1)
                    pool.tensor_tensor(rstd[:, :], var[:, :], c["minus_half"][:, 0:G], ALU.pow).then_inc(s("rstd_ready"), 1)

                @block.scalar
                def _(act):
                    for k in range(DC):
                        act.wait_ge(s("xs_turned"), 4 * (k + 1))
                        act.activation(xt[:, k, :], ps[6 + k][:, :], ACT.Copy).then_inc(s("xt_ready"), 1)
                    feed_forward(None, act, s, ps, xt, w1, w2, ht, None, "act")

                @block.tensor
                def _(pe):
                    pe.wait_ge(s("xs_here"), 16)
                    for k in range(DC):
                        for u in range(G):
                            pe.transpose(ps[6 + k][:, u * P:(u + 1) * P], xs[:, u, k * P:(k + 1) * P],
                                         c["ident"][:, :]).then_inc(s("xs_turned"), 1)
                    feed_forward(pe, None, s, ps, xt, w1, w2, ht, None, "pe")
                    pe.wait_ge(s("sum_ready"), FC)
                    for u in range(G):
                        mm = pe.matmul(ps[6][:, u:u + 1], sum_sq[:, u * P:(u + 1) * P], c["ones"][:, 0:1], start=True, stop=True)
                    mm.then_inc(s("ss_made"), 1)

                @block.vector
                def _(dve):
                    for f in range(FC // 2):
                        dve.wait_ge(s("ht_ready"), f + 1)
                        dve.tensor_tensor(sq[:, f, :], ht[:, f, :], ht[:, f, :], ALU.mult).then_inc(s("sq_ready_a"), 1)
                    dve.wait_ge(s("sq_ready_a"), 2)
                    dve.tensor_tensor(sum_sq[:, :], sq[:, 0, :], sq[:, 1, :], ALU.add).then_inc(s("sum_ready"), 2)
                    for f in range(2, FC):
                        dve.wait_ge(s("sq_ready_a"), min(f + 1, FC // 2))
                        if f >= FC // 2:
                            dve.wait_ge(s("sq_ready_b"), f + 1 - FC // 2)
                        dve.wait_ge(s("sum_ready"), f)
                        dve.tensor_tensor(sum_sq[:, :], sum_sq[:, :], sq[:, f, :], ALU.add).then_inc(s("sum_ready"), 1)
                    dve.wait_ge(s("ss_made"), 1)
                    dve.tensor_scalar(ms[:, :], ps[6][:, 0:G], 1.0 / FF, None, ALU.mult).then_inc(s("ms_ready"), 1)
                    dve.wait_ge(s("rms_ready"), 1)
                    dve.tensor_scalar(rms[:, :], rms[:, :], 1e-8, None, ALU.add).then_inc(s("scale_ready"), 1)
                    dve.wait_ge(s("scale_ready"), 1)
                    dve.reciprocal(rms[:, :], rms[:, :]).then_inc(s("scale_ready"), 1)
                    dve.wait_ge(s("scale_ready"), 2)
                    dve.wait_ge(s("a_here"), 16)
                    dve.wait_ge(s("y_made"), 2)
                    for u in range(G):
                        dve.scalar_tensor_tensor(x1[:, u, :], ps[4 + u // 2][:, (u % 2) * D:(u % 2 + 1) * D], rms[:, u:u + 1],
                                                 a[:, u, :], ALU.mult, ALU.add).then_inc(s("x1_ready"), 1)
                    for u in range(G):
                        dve.wait_ge(s("x1_ready"), u + 1)
                        dve.bn_stats(stats[:, u, :], x1[:, u, :]).then_inc(s("stats_ready"), 1)
                    for u in range(G):
                        dve.wait_ge(s("stats_ready"), u + 1)
                        dve.bn_aggr(mv[:, u, :], stats[:, u, :]).then_inc(s("mv_ready"), 1)
                    dve.wait_ge(s("mv_ready"), G)
                    dve.tensor_scalar(var[:, :], mv[:, :, 1], 1e-5, None, ALU.add).then_inc(s("var_ready"), 1)
                    dve.wait_ge(s("rstd_ready"), 1)
                    for u in range(G):
                        dve.tensor_scalar(xn[:, u, :], x1[:, u, :], mv[:, u, 0:1], rstd[:, u:u + 1], ALU.subtract,
                                          ALU.mult).then_inc(s("xn_ready"), 1)


def experts(pr, io, c):
    nc = pr.nc
    with ExitStack() as ctx:
        def sb(name, shape):
            return ctx.enter_context(nc.sbuf_tensor("e_" + name, shape, F32))

        ps = [ctx.enter_context(nc.psum_tensor(f"e_bank{i}", [P, 512], F32)) for i in range(8)]
        w1, w2 = sb("w1", [P, DC, FF]), sb("w2", [P, FC, D])
        b1, b2 = sb("b1", [P, FC]), sb("b2", [P, D])
        x, y = sb("x", [P, G, D]), sb("y", [P, G, D])
        xt, ht = sb("xt", [P, DC, GT]), sb("ht", [P, FC, GT])
        with nc.Fori(0, E) as e:
            with pr.body() as (block, s):
                @block.sync
                def _(sp):
                    sp.dma_start(w1[:, :, :], io["L1_ffn_W1"][bass.ds(e * D, D), :].rearrange("(c p) n -> p c n", p=P)
                                 ).then_inc(s("w_here"), 16)
                    sp.dma_start(w2[:, :, :], io["L1_ffn_W2"][bass.ds(e * FF, FF), :].rearrange("(c p) n -> p c n", p=P)
                                 ).then_inc(s("w_here"), 16)
                    sp.dma_start(b1[:, :], io["L1_ffn_b1_T"][bass.ds(e * P, P), :]).then_inc(s("w_here"), 16)
                    sp.dma_start(b2[:, :], io["L1_ffn_b2"][bass.ds(e, 1), :].to_broadcast([P, D])).then_inc(s("w_here"), 16)
                    sp.wait_ge(s("w_here"), 64)
            with nc.Fori(0, CAP // GT) as g:
                n = e * (CAP // GT) + g
                with pr.body() as (block, s):
                    @block.sync
                    def _(sp):
                        sp.dma_start(x[:, :, :], rows(io["s_ei"], n, GT)).then_inc(s("x_here"), 16)
                        sp.wait_ge(s("y_ready"), 2)
                        sp.dma_start(rows(io["s_eo"], n, GT), y[:, :, :]).then_inc(s("stored"), 16)
                        sp.wait_ge(s("stored"), 16)

                    @block.scalar
                    def _(act):
                        feed_forward(None, act, s, ps, xt, w1, w2, ht, b1, "act")

                    @block.tensor
                    def _(pe):
                        pe.wait_ge(s("x_here"), 16)
                        for k in range(DC):
                            for u in range(G):
                                pe.transpose(ps[6 + k][:, u * P:(u + 1) * P], x[:, u, k * P:(k + 1) * P],
                                             c["ident"][:, :]).then_inc(s("x_turned"), 1)
                        feed_forward(pe, None, s, ps, xt, w1, w2, ht, b1, "pe")

                    @block.vector
                    def _(dve):
                        for k in range(DC):
                            dve.wait_ge(s("x_turned"), 4 * (k + 1))
                            dve.tensor_copy(xt[:, k, :], ps[6 + k][:, :]).then_inc(s("xt_ready"), 1)
                        for h in range(2):
                            dve.wait_ge(s("y_made"), h + 1)
                            dve.tensor_tensor(y[:, 2 * h:2 * h + 2, :], ps[4 + h][:, :].rearrange("p (g n) -> p g n", g=2),
                                              wide(b2[:, :], 2), ALU.add).then_inc(s("y_ready"), 1)


COLS = ("time_maa_x", "time_maa_rg", "time_maa_wa", "time_maa_k", "time_maa_v", "time_decay", "time_faaaa",
        "time_aaaaa", "time_misc_a", "time_misc_k")
MAA_X, MAA, DECAY, FAAAA, AAAAA = 0, 1, 5, 6, 7
CHN = 5
TOK = 2 * D + HEADS


def recurrence_inputs(pr, io, c):
    nc = pr.nc
    with ExitStack() as ctx:
        def sb(name, shape, dt=F32):
            return ctx.enter_context(nc.sbuf_tensor("r_" + name, shape, dt))

        ps = [ctx.enter_context(nc.psum_tensor(f"r_bank{i}", [P, 512], F32)) for i in range(8)]
        w_mix, w_mix2 = sb("w_mix", [P, DC, P]), sb("w_mix2", [P, D])
        w_r, w_k, w_v = (sb(n, [P, DC, D]) for n in ("w_r", "w_k", "w_v"))
        w_wa, w_lk, w_g = sb("w_wa", [P, DC, P]), sb("w_lk", [P, DC, 64]), sb("w_g", [P, DC, P])
        w_wa2, w_lk2, w_g2 = sb("w_wa2", [P, D]), sb("w_lk2", [64, D]), sb("w_g2", [P, D])
        col = sb("col", [P, len(COLS), DC])
        block_ones, head_sel = sb("block_ones", [P, P]), sb("head_sel", [P, 2])
        x, xt = sb("x", [P, G, D]), sb("xt", [P, DC, GT + 1])
        xx, xm, mi = sb("xx", [P, DC, GT]), sb("xm", [P, DC, GT]), sb("mi", [P, GT])
        xf = [sb(f"xf{i}", [P, DC, GT]) for i in range(4)]
        k, kk, a, ma, mk = (sb(n, [P, DC, GT]) for n in ("k", "kk", "a", "ma", "mk"))
        sp_e, low, t = sb("sp_e", [P, DC, GT]), sb("low", [P, DC, GT]), sb("t", [P, DC, GT])
        la, lk, gh = sb("la", [P, GT]), sb("lk", [64, GT]), sb("gh", [P, GT])
        chn = sb("chn", [P, CHN, DC, GT])
        tok = sb("tok", [P, G, TOK])
        with pr.body() as (block, s):
            @block.gpsimd
            def _(pool):
                pool.memset(w_wa[:, :, :], 0.0).then_inc(s("zeroed"), 1)
                pool.memset(w_lk[:, :, :], 0.0).then_inc(s("zeroed"), 1)
                pool.memset(block_ones[:, :], 0.0).then_inc(s("zeroed"), 1)
                pool.memset(head_sel[:, :], 0.0).then_inc(s("zeroed"), 1)
                pool.memset(w_wa2[:, :], 0.0).then_inc(s("zeroed"), 1)
                pool.memset(w_lk2[:, :], 0.0).then_inc(s("zeroed"), 1)
                pool.wait_ge(s("zeroed"), 6)
                for h in range(2):
                    pool.memset(block_ones[h * 64:h * 64 + 64, h * 64:h * 64 + 64], 1.0)
                    pool.memset(head_sel[h * 64:h * 64 + 64, h:h + 1], 1.0)

            @block.sync
            def _(sp):
                def cols(name):
                    return io["L1_attn_" + name].rearrange("(c p) n -> p c n", p=P)

                loads = [(w_mix[:, :, :], cols("time_maa_w1")), (w_mix2[:, :], io["L1_attn_time_maa_w2"]),
                         (w_r[:, :, :], cols("w_receptance_T")), (w_k[:, :, :], cols("w_key_T")),
                         (w_v[:, :, :], cols("w_value_T")), (w_g[:, :, :], cols("gate_w1")),
                         (w_g2[:, :], io["L1_attn_gate_w2"])]
                loads.append((col[:, :, :].rearrange("p i c -> p (i c)"), io["L1_attn_columns"]))
                packed = [(w_wa[:, :, 0:64], cols("time_decay_w1")), (w_wa[:, :, 64:80], cols("time_aaa_w1")),
                          (w_wa[:, :, 96:112], cols("ma_w1")), (w_lk[:, :, 0:16], cols("time_kkk_w1")),
                          (w_lk[:, :, 32:48], cols("mk_w1")), (w_wa2[0:64, :], io["L1_attn_time_decay_w2"]),
                          (w_wa2[64:80, :], io["L1_attn_time_aaa_w2"]), (w_wa2[96:112, :], io["L1_attn_ma_w2"]),
                          (w_lk2[0:16, :], io["L1_attn_time_kkk_w2"]), (w_lk2[32:48, :], io["L1_attn_mk_w2"])]
                for out, src in loads:
                    sp.dma_start(out, src).then_inc(s("w_here"), 16)
                sp.wait_ge(s("zeroed"), 6)
                for out, src in packed:
                    sp.dma_start(out, src).then_inc(s("w_here"), 16)
                sp.wait_ge(s("w_here"), 16 * (len(loads) + len(packed)))

            @block.vector
            def _(dve):
                dve.wait_ge(s("w_here"), 16 * (8 + 10))
                dve.tensor_scalar(col[:, AAAAA:AAAAA + 3, :], col[:, AAAAA:AAAAA + 3, :], -1.0, None, ALU.mult)

        with nc.Fori(0, B) as b:
            with pr.body() as (block, s):
                @block.vector
                def _(dve):
                    dve.memset(xt[:, :, GT:GT + 1], 0.0)
            with nc.Fori(0, S // GT) as g:
                n = b * (S // GT) + g
                with pr.body() as (block, s):
                    @block.sync
                    def _(sp):
                        sp.dma_start(x[:, :, :], rows(io["s_xn"], n, GT)).then_inc(s("x_here"), 16)
                        sp.wait_ge(s("tok_ready"), 5)
                        sp.dma_start(io["s_tok"][bass.ds(n * P, P), :], tok[:, :, :].rearrange("p g n -> p (g n)")).then_inc(s("stored"), 16)
                        sp.wait_ge(s("r_ready"), 2)
                        sp.wait_ge(s("w_ready"), 1)
                        sp.wait_ge(s("k2_ready"), 1)
                        sp.wait_ge(s("na_ready"), 1)
                        sp.wait_ge(s("b_ready"), 1)
                        sp.dma_start(io["s_ch"][bass.ds(n * P, P), :], chn[:, :, :, :].rearrange("p i c n -> p (i c n)")).then_inc(s("stored"), 16)
                        sp.wait_ge(s("stored"), 32)

                    @block.tensor
                    def _(pe):
                        pe.wait_ge(s("x_here"), 16)
                        for i in range(DC):
                            for u in range(G):
                                pe.transpose(ps[i][:, u * P:(u + 1) * P], x[:, u, i * P:(i + 1) * P],
                                             c["ident"][:, :]).then_inc(s("x_turned"), 1)
                        pe.wait_ge(s("xm_ready"), DC)
                        for i in range(DC):
                            mm = pe.matmul(ps[2][:, :], w_mix[:, i, :], xm[:, i, :], start=i == 0, stop=i == DC - 1)
                        mm.then_inc(s("mi_made"), 1)
                        pe.wait_ge(s("mi_ready"), 1)
                        for i in range(DC):
                            for f in range(4):
                                if i:
                                    pe.wait_ge(s("mix_used"), f + 1)
                                pe.matmul(ps[3 + f][:, :], w_mix2[32 * f:32 * f + 32, i * P:(i + 1) * P], mi[32 * f:32 * f + 32, :],
                                          start=True, stop=True, tile_position=(32 * f, 0)).then_inc(s("mix_made"), 1)
                        pe.wait_ge(s("xf_ready"), 4 * DC)
                        pe.wait_ge(s("xt_ready"), DC)

                        def product(bank, w, src, cols, name, m=P):
                            for i in range(DC):
                                mm = pe.matmul(bank[0:m, :], w[:, i, cols], src[:, i, :], start=i == 0, stop=i == DC - 1)
                            mm.then_inc(s(name), 1)

                        product(ps[0], w_g, xf[0], slice(0, P), "gh_made")
                        product(ps[1], w_wa, xf[1], slice(0, P), "la_made")
                        product(ps[2], w_lk, xf[2], slice(0, 64), "lk_made", 64)
                        for i in range(DC):
                            product(ps[3 + i], w_r, xf[0], slice(i * P, (i + 1) * P), "r_made")
                        for i in range(DC):
                            product(ps[5 + i], w_k, xf[2], slice(i * P, (i + 1) * P), "k_made")

                        def second(bank, w, src, lo, hi, i, name):
                            pe.matmul(bank[:, :], w[lo:hi, i * P:(i + 1) * P], src[lo:hi, :], start=True, stop=True,
                                      tile_position=(lo, 0)).then_inc(s(name), 1)

                        pe.wait_ge(s("gh_ready"), 1)
                        pe.wait_ge(s("la_ready"), 2)
                        for i in range(DC):
                            second(ps[i], w_wa2, la, 0, 64, i, "z_made")
                        pe.wait_ge(s("lk_ready"), 2)
                        pe.wait_ge(s("r_ready"), 1)
                        for i in range(DC):
                            second(ps[2 + i], w_wa2, la, 64, 80, i, "a_made")
                        pe.wait_ge(s("r_ready"), 2)
                        pe.wait_ge(s("k_ready"), 2)
                        for i in range(DC):
                            second(ps[4 + i], w_wa2, la, 96, 112, i, "ma_made")
                        for i in range(DC):
                            second(ps[6 + i], w_lk2, lk, 0, 16, i, "kkk_made")
                        pe.wait_ge(s("z_used"), 2 * DC)
                        for i in range(DC):
                            second(ps[i], w_lk2, lk, 32, 48, i, "mk_made")
                        pe.wait_ge(s("kk2_ready"), 1)
                        pe.wait_ge(s("a_exp"), DC)
                        for i in range(DC):
                            pe.matmul(ps[2 + i][:, :], block_ones[:, :], t[:, i, :], start=True, stop=True).then_inc(s("ss_made"), 1)
                        pe.wait_ge(s("ma_exp"), DC)
                        for u in range(G):
                            for i in range(DC):
                                mm = pe.matmul(ps[4 + u // 2][:, (u % 2) * D:(u % 2 + 1) * D], xf[3][:, i, u * P:(u + 1) * P],
                                               w_v[:, i, :], start=i == 0, stop=i == DC - 1)
                            if u % 2:
                                mm.then_inc(s("v_made"), 1)
                        pe.wait_ge(s("kk_ready"), DC)
                        for u in range(G):
                            mm = pe.matmul(ps[6 + u // 2][:, (u % 2) * D:(u % 2 + 1) * D], gh[:, u * P:(u + 1) * P], w_g2[:, :],
                                           start=True, stop=True)
                            if u % 2:
                                mm.then_inc(s("g_made"), 1)
                        pe.wait_ge(s("rkf_ready"), DC)
                        pe.wait_ge(s("mk_exp"), DC)
                        for u in range(G):
                            for i in range(DC):
                                mm = pe.matmul(ps[0][:, u * HEADS + 2 * i:u * HEADS + 2 * i + 2], sp_e[:, i, u * P:(u + 1) * P], head_sel[:, :],
                                               start=True, stop=True)
                        mm.then_inc(s("bonus_made"), 1)

                    @block.scalar
                    def _(act):
                        act.activation(xt[:, :, 0:1], xt[:, :, GT:GT + 1], ACT.Copy).then_inc(s("prev_ready"), 1)
                        act.wait_ge(s("prev_ready"), 1)
                        for i in range(DC):
                            act.wait_ge(s("x_turned"), 4 * (i + 1))
                            act.activation(xt[:, i, 1:GT + 1], ps[i][:, :], ACT.Copy).then_inc(s("xt_ready"), 1)
                        act.wait_ge(s("mi_made"), 1)
                        act.activation(mi[:, :], ps[2][:, :], ACT.Tanh).then_inc(s("mi_ready"), 1)
                        act.wait_ge(s("gh_made"), 1)
                        act.activation(gh[:, :], ps[0][:, :], ACT.Tanh).then_inc(s("gh_ready"), 1)
                        act.wait_ge(s("la_made"), 1)
                        act.activation(la[0:64, :], ps[1][0:64, :], ACT.Tanh).then_inc(s("la_ready"), 1)
                        act.activation(la[64:128, :], ps[1][64:128, :], ACT.Copy).then_inc(s("la_ready"), 1)
                        act.wait_ge(s("lk_made"), 1)
                        act.activation(lk[0:32, :], ps[2][0:32, :], ACT.Tanh).then_inc(s("lk_ready"), 1)
                        act.activation(lk[32:64, :], ps[2][32:64, :], ACT.Copy).then_inc(s("lk_ready"), 1)
                        for i in range(DC):
                            act.wait_ge(s("r_made"), i + 1)
                            act.activation(chn[:, 0, i, :], ps[3 + i][:, :], ACT.Copy).then_inc(s("r_ready"), 1)
                        for i in range(DC):
                            act.wait_ge(s("a_made"), i + 1)
                            act.activation(a[:, i, :], ps[2 + i][:, :], ACT.Exp, bias=col[:, AAAAA, i:i + 1], scale=-1.0).then_inc(s("a_exp"), 1)
                        for i in range(DC):
                            act.wait_ge(s("ma_made"), i + 1)
                            act.activation(ma[:, i, :], ps[4 + i][:, :], ACT.Exp, bias=col[:, AAAAA + 1, i:i + 1], scale=-1.0).then_inc(s("ma_exp"), 1)
                        for i in range(DC):
                            act.wait_ge(s("mk_made"), i + 1)
                            act.activation(mk[:, i, :], ps[i][:, :], ACT.Exp, bias=col[:, AAAAA + 2, i:i + 1], scale=-1.0).then_inc(s("mk_exp"), 1)
                        act.wait_ge(s("z_abs"), 1)
                        act.activation(sp_e[:, :, :], sp_e[:, :, :], ACT.Exp, scale=-1.0).then_inc(s("softplus"), 1)
                        act.wait_ge(s("softplus"), 1)
                        act.activation(sp_e[:, :, :], sp_e[:, :, :], ACT.Ln, bias=1.0).then_inc(s("softplus"), 1)
                        act.wait_ge(s("ss_ready"), DC)
                        act.activation(t[:, :, :], t[:, :, :], ACT.Ln).then_inc(s("norm"), 1)
                        act.wait_ge(s("norm"), 1)
                        act.activation(t[:, :, :], t[:, :, :], ACT.Exp, scale=-0.5).then_inc(s("norm"), 1)
                        act.wait_ge(s("wm_ready"), 1)
                        act.activation(mk[:, :, :], mk[:, :, :], ACT.Exp).then_inc(s("decay_ready"), 1)
                        for h in range(2):
                            act.wait_ge(s("g_made"), h + 1)
                            act.activation(tok[:, 2 * h:2 * h + 2, D:2 * D], ps[6 + h][:, :].rearrange("p (g n) -> p g n", g=2),
                                           ACT.Copy).then_inc(s("tok_ready"), 1)
                        for h in range(2):
                            act.wait_ge(s("v_made"), h + 1)
                            act.activation(tok[:, 2 * h:2 * h + 2, 0:D], ps[4 + h][:, :].rearrange("p (g n) -> p g n", g=2),
                                           ACT.Copy).then_inc(s("tok_ready"), 1)

                    @block.gpsimd
                    def _(pool):
                        for i in range(DC):
                            for f in range(4):
                                pool.wait_ge(s("mix_used"), 4 * i + f + 1)
                                pool.tensor_tensor(xf[f][:, i, :], xf[f][:, i, :], xt[:, i, 1:GT + 1], ALU.add).then_inc(s("xf_ready"), 1)
                        for m, (z, name) in enumerate(((a, "a_exp"), (ma, "ma_exp"))):
                            pool.wait_ge(s(name), DC)
                            pool.tensor_scalar(z[:, :, :], z[:, :, :], 1.0, None, ALU.add).then_inc(s("plus_one"), 1)
                        pool.wait_ge(s("kk_ready"), DC)
                        pool.tensor_tensor(t[:, :, :], kk[:, :, :], kk[:, :, :], ALU.mult).then_inc(s("kk2_ready"), 1)
                        pool.wait_ge(s("mk_exp"), DC)
                        pool.tensor_scalar(mk[:, :, :], mk[:, :, :], 1.0, None, ALU.add).then_inc(s("plus_one"), 1)

                    @block.vector
                    def _(dve):
                        dve.wait_ge(s("prev_ready"), 1)
                        for i in range(DC):
                            dve.wait_ge(s("xt_ready"), i + 1)
                            dve.tensor_tensor(xx[:, i, :], xt[:, i, 0:GT], xt[:, i, 1:GT + 1], ALU.subtract).then_inc(s("xx_ready"), 1)
                        for i in range(DC):
                            dve.wait_ge(s("xx_ready"), i + 1)
                            dve.scalar_tensor_tensor(xm[:, i, :], xx[:, i, :], col[:, MAA_X, i:i + 1], xt[:, i, 1:GT + 1],
                                                     ALU.mult, ALU.add).then_inc(s("xm_ready"), 1)
                        for i in range(DC):
                            for f in range(4):
                                dve.wait_ge(s("mix_made"), 4 * i + f + 1)
                                dve.scalar_tensor_tensor(xf[f][:, i, :], ps[3 + f][:, :], col[:, MAA + f, i:i + 1], xx[:, i, :],
                                                         ALU.add, ALU.mult).then_inc(s("mix_used"), 1)
                        for i in range(DC):
                            dve.wait_ge(s("k_made"), i + 1)
                            dve.tensor_copy(k[:, i, :], ps[5 + i][:, :]).then_inc(s("k_ready"), 1)
                        for i in range(DC):
                            dve.wait_ge(s("z_made"), i + 1)
                            dve.tensor_scalar(sp_e[:, i, :], ps[i][:, :], col[:, DECAY, i:i + 1], 0.0, ALU.add, ALU.max).then_inc(s("z_used"), 1)
                            dve.tensor_scalar(low[:, i, :], ps[i][:, :], col[:, DECAY, i:i + 1], 0.0, ALU.add, ALU.min).then_inc(s("z_used"), 1)
                        dve.wait_ge(s("z_used"), 2 * DC)
                        dve.tensor_tensor(sp_e[:, :, :], sp_e[:, :, :], low[:, :, :], ALU.subtract).then_inc(s("z_abs"), 1)
                        dve.wait_ge(s("k_ready"), DC)
                        for i in range(DC):
                            dve.wait_ge(s("kkk_made"), i + 1)
                            dve.tensor_tensor(kk[:, i, :], ps[6 + i][:, :], k[:, i, :], ALU.add).then_inc(s("kk_ready"), 1)
                        for m, z in enumerate((a, ma)):
                            dve.wait_ge(s("plus_one"), m + 1)
                            dve.reciprocal(z[:, :, :], z[:, :, :]).then_inc(s("sigmoid"), 1)
                        for i in range(DC):
                            dve.wait_ge(s("ss_made"), i + 1)
                            dve.tensor_scalar(t[:, i, :], ps[2 + i][:, :], 1e-24, None, ALU.max).then_inc(s("ss_ready"), 1)
                        dve.wait_ge(s("softplus"), 2)
                        dve.scalar_tensor_tensor(chn[:, 1, :, :], low[:, :, :], -0.5, sp_e[:, :, :], ALU.add, ALU.subtract).then_inc(s("w_ready"), 1)
                        dve.wait_ge(s("plus_one"), 3)
                        dve.reciprocal(mk[:, :, :], mk[:, :, :]).then_inc(s("sigmoid"), 1)
                        dve.wait_ge(s("sigmoid"), 3)
                        dve.wait_ge(s("w_ready"), 1)
                        dve.tensor_tensor(mk[:, :, :], mk[:, :, :], chn[:, 1, :, :], ALU.mult).then_inc(s("wm_made"), 1)
                        dve.tensor_scalar(low[:, :, :], ma[:, :, :], -1.0, 1.0, ALU.mult, ALU.add).then_inc(s("mix_a"), 1)
                        dve.wait_ge(s("wm_made"), 1)
                        dve.tensor_scalar(mk[:, :, :], mk[:, :, :], 0.0, None, ALU.min).then_inc(s("wm_ready"), 1)
                        dve.wait_ge(s("mix_a"), 1)
                        dve.tensor_tensor(low[:, :, :], low[:, :, :], a[:, :, :], ALU.mult).then_inc(s("mix_a"), 1)
                        dve.wait_ge(s("mix_a"), 2)
                        dve.tensor_tensor(low[:, :, :], low[:, :, :], ma[:, :, :], ALU.add).then_inc(s("mix_a"), 1)
                        dve.wait_ge(s("mix_a"), 3)
                        dve.tensor_tensor(k[:, :, :], k[:, :, :], low[:, :, :], ALU.mult).then_inc(s("mix_a"), 1)
                        dve.wait_ge(s("norm"), 2)
                        dve.tensor_tensor(kk[:, :, :], kk[:, :, :], t[:, :, :], ALU.mult).then_inc(s("kkn_ready"), 1)
                        dve.wait_ge(s("kkn_ready"), 1)
                        dve.tensor_scalar(chn[:, 3, :, :], kk[:, :, :], -1.0, None, ALU.mult).then_inc(s("na_ready"), 1)
                        dve.tensor_tensor(chn[:, 4, :, :], kk[:, :, :], a[:, :, :], ALU.mult).then_inc(s("b_ready"), 1)
                        dve.wait_ge(s("mix_a"), 4)
                        dve.wait_ge(s("decay_ready"), 1)
                        dve.tensor_tensor(chn[:, 2, :, :], k[:, :, :], mk[:, :, :], ALU.mult).then_inc(s("k2_ready"), 1)
                        dve.wait_ge(s("k2_ready"), 1)
                        dve.wait_ge(s("r_ready"), 2)
                        for i in range(DC):
                            dve.scalar_tensor_tensor(sp_e[:, i, :], chn[:, 0, i, :], col[:, FAAAA, i:i + 1], chn[:, 2, i, :],
                                                     ALU.mult, ALU.mult).then_inc(s("rkf_ready"), 1)
                        dve.wait_ge(s("bonus_made"), 1)
                        dve.tensor_copy(tok[:, :, 2 * D:TOK], ps[0][:, 0:G * HEADS].rearrange("p (g n) -> p g n", g=G)).then_inc(s("tok_ready"), 1)


LEVELS = (16, 8, 4, 2, 1)
POWERS_FROM = (0, 0, 0, 1, 2)


def recurrence(pr, io, c):
    nc = pr.nc
    NCH = GT // CH
    with ExitStack() as ctx:
        def sb(name, shape, dt=F32):
            return ctx.enter_context(nc.sbuf_tensor("q_" + name, shape, dt))

        ps = [ctx.enter_context(nc.psum_tensor(f"q_bank{i}", [P, 512], F32)) for i in range(8)]
        w_o = sb("w_o", [P, DC, D])
        lnw, lnb = sb("lnw", [P, D]), sb("lnb", [P, D])
        not_first = sb("not_first", [P, GT])
        ident2 = sb("ident2", [P, HN])
        mask_f = sb("mask_f", [P, P])
        masks = [sb(f"mask{i}", [P, CH], U32) for i in range(len(LEVELS) + 1)]
        eye = sb("eye", [P, CH])
        chn, tok = sb("chn", [P, CHN, DC, GT]), sb("tok", [P, G, TOK])
        wc = sb("wc", [P, DC * GT])
        dd = sb("dd", [P, 2, 3, GT])
        ar = sb("ar", [P, 2, 2, DC, GT // 2])
        ar_s = [ar[:, i, :, :, :] for i in range(2)]
        a_end = ar[:, 1, :, :, :].rearrange("p a c n -> p (a c n)").rearrange("p (c n) -> p c n", c=DC)
        bk_s = [sb(f"bk_s{i}", [P, 2, DC, GT]) for i in range(2)]
        rt, dl = sb("rt", [P, DC, GT]), sb("dl", [P, DC * NCH])
        tm = sb("tm", [P, G, 3, D])
        at = sb("at", [P, 2, G * DC, 4, CH])
        bai = sb("bai", [P, G, 3, HEADS, CH])
        xq = sb("xq", [P, G, HEADS, HN])
        pq = sb("pq", [P, G, HEADS, 2 * HN])
        dg = sb("dg", [P, G, DC * QN, HN])
        rp = sb("rp", [P, G, DC, P])
        mt = ar[:, :, :, :, :].rearrange("p i a c n -> p (i a c n)").rearrange("p (u c q n) -> p u c q n", u=G, c=DC, q=QN)
        cc = bk_s[0][:, :, :, :].rearrange("p a c n -> p (a c n)").rearrange("p (u c q n) -> p u c q n", u=G, c=DC, q=QN)
        st = sb("st", [P, NCH + 1, DC, HN])
        y, x1 = sb("y", [P, G, D]), sb("x1", [P, G, D])
        yt = rt
        stats, mv = sb("stats", [P, G * HEADS, 6]), sb("mv", [P, G * HEADS, 2])
        var, rstd = sb("var", [P, G * HEADS]), sb("rstd", [P, G * HEADS])

        def halves(ap, n):
            return ap.rearrange("p (b h n) -> p b h n", h=2, n=n)

        with pr.body() as (block, s):
            @block.sync
            def _(sp):
                sp.dma_start(w_o[:, :, :], io["L1_attn_w_output_T"].rearrange("(c p) n -> p c n", p=P)).then_inc(s("w_here"), 16)
                sp.dma_start(lnw[:, :], io["L1_attn_ln_w"].rearrange("(a n) -> a n", a=1).to_broadcast([P, D])).then_inc(s("w_here"), 16)
                sp.dma_start(lnb[:, :], io["L1_attn_ln_b"].rearrange("(a n) -> a n", a=1).to_broadcast([P, D])).then_inc(s("w_here"), 16)
                sp.wait_ge(s("w_here"), 48)

            @block.scalar
            def _(act):
                for i in range(len(LEVELS) + 1):
                    act.wait_ge(s("mask_made"), i + 1)
                    for q in range(QN):
                        row = slice(CH * q, CH * (q + 1))
                        act.activation(masks[i][row, :], mask_f[row, CH * q:CH * (q + 1)], ACT.Copy).then_inc(s("mask_read"), 1)

            @block.gpsimd
            def _(pool):
                k = 0

                def step(ins):
                    nonlocal k
                    ins.then_inc(s("pool_step"), 1)
                    k += 1
                    pool.wait_ge(s("pool_step"), k)

                for i, n in enumerate(LEVELS):
                    if i:
                        pool.wait_ge(s("mask_read"), QN * i)
                    m = mask_f[:, :].rearrange("p (b h n) -> p b h n", h=2, n=n)
                    step(pool.memset(mask_f[:, :], 0.0))
                    step(pool.memset(m[:, :, 1, :], 1.0))
                    step(pool.affine_select(out=m[:, :, 1, :], in_=m[:, :, 1, :], compare_op=ALU.is_ge, fill=0.0, base=0,
                                            pattern=[[-2 * n, P // (2 * n)], [0, n]], channel_multiplier=1))
                    pool.affine_select(out=m[:, :, 1, :], in_=m[:, :, 1, :], compare_op=ALU.is_ge, fill=0.0, base=n - 1,
                                       pattern=[[2 * n, P // (2 * n)], [0, n]], channel_multiplier=-1).then_inc(s("mask_made"), 1)
                pool.wait_ge(s("mask_read"), QN * len(LEVELS))
                pool.tensor_copy(mask_f[:, :], c["ident"][:, :]).then_inc(s("mask_made"), 1)
                pool.wait_ge(s("mask_made"), len(LEVELS) + 1)
                for q in range(QN):
                    step(pool.tensor_copy(eye[CH * q:CH * (q + 1), :], c["ident"][CH * q:CH * (q + 1), CH * q:CH * (q + 1)]))
                step(pool.memset(not_first[:, :], 1.0))
                step(pool.memset(not_first[:, :].rearrange("p (q n) -> p q n", n=CH)[:, :, 0:1], 0.0))
                step(pool.tensor_tensor(ident2[:, :], c["ident"][:, 0:HN], c["ident"][:, HN:2 * HN], ALU.add))

            @block.vector
            def _(dve):
                for i in range(2):
                    dve.memset(bk_s[i][:, :, :, :], 0.0)
                dve.memset(at[:, :, :, :, :], 0.0)
                dve.memset(bai[:, :, :, :, :], 0.0)

        with nc.Fori(0, B) as b:
            with pr.body() as (block, s):
                @block.vector
                def _(dve):
                    dve.memset(st[:, NCH, :, :], 0.0)
            with nc.Fori(0, S // GT) as g:
                n_ = b * (S // GT) + g
                with pr.body() as (block, s):
                    @block.sync
                    def _(sp):
                        for i, name in ((1, "w_here"), (3, "a_here"), (4, "b_here"), (2, "k_here"), (0, "r_here")):
                            sp.dma_start(chn[:, i, :, :].rearrange("p c n -> p (c n)"),
                                         io["s_ch"][bass.ds(n_ * P, P), DC * GT * i:DC * GT * (i + 1)]).then_inc(s(name), 16)
                        sp.dma_start(tok[:, :, :].rearrange("p g n -> p (g n)"), io["s_tok"][bass.ds(n_ * P, P), :]).then_inc(s("tok_here"), 16)
                        sp.dma_start(x1[:, :, :], rows(io["s_x1"], n_, GT)).then_inc(s("x1_here"), 16)
                        sp.wait_ge(s("out_ready"), 2)
                        sp.dma_start(rows(io["s_rw"], n_, GT), x1[:, :, :]).then_inc(s("stored"), 16)
                        sp.wait_ge(s("stored"), 16)

                    @block.scalar
                    def _(act):
                        flat = dd[:, :, :, :].rearrange("p a b n -> p (a b n)")
                        act.wait_ge(s("ends_ready"), 2)
                        act.activation(flat[:, 0:4 * GT], flat[:, 0:4 * GT], ACT.Exp).then_inc(s("end_exp"), 1)
                        act.activation(flat[:, 4 * GT:6 * GT], wc[:, :], ACT.Exp).then_inc(s("end_exp"), 1)

                        def level_exp(i):
                            act.wait_ge(s("dd_ready"), 3 * (i + 1))
                            act.activation(dd[:, i % 2, :, :], dd[:, i % 2, :, :], ACT.Exp).then_inc(s("dd_exp"), 1)

                        level_exp(0)
                        for u in range(G):
                            act.wait_ge(s("tm_made"), u + 1)
                            act.activation(tm[:, u, 0:2, :], ps[2 * (u % 2)][:, :].rearrange("p (a n) -> p a n", a=2), ACT.Copy).then_inc(s("tm_ready"), 1)
                            act.activation(tm[:, u, 2, :], ps[2 * (u % 2) + 1][:, 0:D], ACT.Copy).then_inc(s("tm_ready"), 1)
                        for i in range(1, len(LEVELS)):
                            level_exp(i)

                        for u in range(G):
                            act.wait_ge(s("fill_made"), u + 1)
                            for q in range(QN // 2):
                                row, bank = slice(CH * q, CH * (q + 1)), ps[4 * (u % 2) + q]
                                act.activation(bai[row, u, 0:2, :, :].rearrange("p a h n -> p (a h n)"), bank[row, 0:2 * P],
                                               ACT.Copy).then_inc(s("fill_read_a"), 1)
                                act.activation(xq[row, u, :, :].rearrange("p h n -> p (h n)"), bank[row, 2 * P:4 * P],
                                               ACT.Copy).then_inc(s("fill_read_a"), 1)
                        for u in range(G):
                            act.wait_ge(s("pq_made"), u + 1)
                            for q in range(QN // 2):
                                row = slice(CH * q, CH * (q + 1))
                                act.activation(pq[row, u, :, :].rearrange("p h n -> p (h n)"), ps[4 * (u % 2) + q][row, :],
                                               ACT.Copy).then_inc(s("pq_ready_a"), 1)
                        for k in range(DC):
                            act.wait_ge(s("y_turned"), 4 * (k + 1))
                            act.activation(yt[:, k, :], ps[4 + k][:, :], ACT.Copy).then_inc(s("yt_ready"), 1)

                    @block.gpsimd
                    def _(pool):
                        flat = dd[:, :, :, :].rearrange("p a b n -> p (a b n)")
                        ends = flat[:, 2 * GT:4 * GT].rearrange("p (c n) -> p c n", c=DC)
                        pool.wait_ge(s("end_exp"), 2)
                        pool.wait_ge(s("b_here"), 16)
                        pool.wait_ge(s("k_here"), 16)
                        pool.tensor_tensor(bk_s[1][:, 0, :, :], chn[:, 4, :, :], ends, ALU.mult).then_inc(s("bk_end"), 1)
                        pool.tensor_tensor(bk_s[1][:, 1, :, :], chn[:, 2, :, :], ends, ALU.mult).then_inc(s("bk_end"), 1)
                        pool.tensor_copy(dl[:, :], flat[:, 4 * GT:6 * GT].rearrange("p (q n) -> p q n", n=CH)[:, :, CH - 1]).then_inc(s("bk_end"), 1)
                        for i, n in enumerate(LEVELS):
                            pool.wait_ge(s("dd_exp"), i + 1)
                            if i == 1:
                                pool.wait_ge(s("tm_made"), G)
                            if i >= 2:
                                pool.wait_ge(s("level_made"), 2 * (i - 1))
                            e = dd[:, i % 2, 0, :].rearrange("p (b n) -> p b n", n=n)
                            for j, src in enumerate((4, 2)):
                                pool.tensor_tensor(halves(bk_s[i % 2][:, j, :, :].rearrange("p c n -> p (c n)"), n)[:, :, 0, :],
                                                   halves(chn[:, src, :, :].rearrange("p c n -> p (c n)"), n)[:, :, 0, :], e,
                                                   ALU.mult).then_inc(s("bk_ready"), 1)
                        pool.wait_ge(s("bk_end"), 3)
                        for u in range(G):
                            for i in range(DC):
                                pool.tensor_tensor(dg[:, u, QN * i:QN * i + QN, :], wide(ident2[:, :], QN),
                                                   dl[:, NCH * i + QN * u:NCH * i + QN * u + QN].unsqueeze(2).to_broadcast([P, QN, HN]),
                                                   ALU.mult).then_inc(s("dg_ready"), 1)
                        pool.wait_ge(s("var_ready"), 1)
                        pool.tensor_tensor(rstd[:, :], var[:, :], c["minus_half"][:, :], ALU.pow).then_inc(s("rstd_ready"), 1)

                    @block.tensor
                    def _(pe):
                        for u in range(G):
                            if u == 0:
                                pe.wait_ge(s("a_end"), 1)
                                pe.wait_ge(s("bk_end"), 2)
                            if u >= 2:
                                pe.wait_ge(s("tm_ready"), 2 * (u - 1))
                            cut = slice(u * P, (u + 1) * P)
                            for i in range(DC):
                                pe.transpose(ps[2 * (u % 2)][:, i * P:(i + 1) * P], a_end[:, i, cut], c["ident"][:, :])
                                pe.transpose(ps[2 * (u % 2)][:, D + i * P:D + (i + 1) * P], bk_s[1][:, 0, i, cut], c["ident"][:, :])
                            for i in range(DC):
                                mm = pe.transpose(ps[2 * (u % 2) + 1][:, i * P:(i + 1) * P], bk_s[1][:, 1, i, cut], c["ident"][:, :])
                            mm.then_inc(s("tm_made"), 1)
                        pe.wait_ge(s("tm_ready"), 2 * G)
                        for i in range(len(LEVELS) + 1):
                            last = i == len(LEVELS)
                            if not last:
                                pe.wait_ge(s("ar_ready"), 2 * (i + 1))
                                pe.wait_ge(s("bk_ready"), 2 * (i + 1))
                            for par in range(2):
                                lo, bank = HN * par, ps[(2 * i + par) % 8]
                                if i >= 4:
                                    pe.wait_ge(s("at_ready"), 2 * (i - 4) + par + 1)
                                for uc in range(G * DC):
                                    u, ci = uc // DC, uc % DC
                                    for q in range(QN):
                                        t = u * P + q * CH
                                        for j, raw in enumerate((4, 2)):
                                            o = bank[CH * q:CH * (q + 1), 2 * CH * uc + j * CH:2 * CH * uc + (j + 1) * CH]
                                            if last:
                                                mm = pe.matmul(o, chn[lo:lo + HN, raw, ci, t:t + CH], chn[lo:lo + HN, 0, ci, t:t + CH],
                                                               start=True, stop=True, tile_position=(lo, CH * q))
                                            else:
                                                mm = pe.matmul(o, bk_s[i % 2][lo:lo + HN, j, ci, t:t + CH],
                                                               ar_s[i % 2][lo:lo + HN, :, ci, t // 2:(t + CH) // 2],
                                                               start=True, stop=True, tile_position=(lo, CH * q))
                                mm.then_inc(s("level_made"), 1)
                        pe.wait_ge(s("at_ready"), 2 * (len(LEVELS) + 1))
                        pe.wait_ge(s("tok_here"), 16)

                        def read_by_dve(n):
                            return sum(QN * (2 if G <= m < 4 * G else 1) for m in range(n + 1))

                        def each(u, body):
                            for q in range(QN):
                                for h in range(HEADS):
                                    mm = body(q, slice(CH * q, CH * (q + 1)), ps[4 * (u % 2) + q], h, (h % 2, DC * u + h // 2))
                            return mm

                        for step in range(5):
                            for u in range(G):
                                def fill(q, row, bank, h, m):
                                    at_q, pos = at[row, m[0], m[1], 0, :], (CH * q, CH * q)
                                    power = at_q if step == 0 else bai[row, u, 0, h, :]
                                    turned = bai[row, u, 1, h, :]
                                    cols = [slice(P * a + CH * h, P * a + CH * (h + 1)) for a in range(3)]
                                    if step < 3:
                                        mm = pe.matmul(bank[row, cols[0]], turned, power, start=True, stop=True, tile_position=pos)
                                    if step < 4:
                                        mm = pe.matmul(bank[row, cols[1]], power, turned, start=True, stop=True, tile_position=pos)
                                    if step:
                                        mm = pe.matmul(bank[row, cols[2]], turned, bai[row, u, 2, h, :], start=True, stop=True, tile_position=pos)
                                    else:
                                        mm = pe.matmul(bank[row, 2 * P + h * HN:2 * P + (h + 1) * HN], at[row, m[0], m[1], 2, :],
                                                       tok[row, u, h * HN:(h + 1) * HN], start=True, stop=True, tile_position=pos)
                                    return mm

                                if step == 0:
                                    pe.wait_ge(s("turned_ready"), 2 * (u + 1))
                                n = G * step + u
                                if n >= 2:
                                    pe.wait_ge(s("fill_read_a"), QN * min(n - 1, G))
                                    pe.wait_ge(s("fill_read_b"), read_by_dve(n - 2))
                                if step == 1:
                                    pe.wait_ge(s("inv_ready"), u + 1)
                                each(u, fill).then_inc(s("fill_made"), 1)
                        for u in range(G):
                            pe.wait_ge(s("fill_read_b"), read_by_dve(min(4 * G + u + 2, 5 * G - 1)))
                            if u >= 2:
                                for name in ("pq_ready_a", "pq_ready_b"):
                                    pe.wait_ge(s(name), QN // 2 * (u - 1))

                            def solve(q, row, bank, h, m):
                                pos = (CH * q, CH * q)
                                pe.matmul(bank[row, 2 * h * HN:(2 * h + 1) * HN], bai[row, u, 2, h, :], tm[row, u, 0, h * HN:(h + 1) * HN],
                                          start=True, stop=True, tile_position=pos)
                                return pe.matmul(bank[row, (2 * h + 1) * HN:(2 * h + 2) * HN], bai[row, u, 2, h, :], xq[row, u, h, :],
                                                 start=True, stop=True, tile_position=pos)

                            each(u, solve).then_inc(s("pq_made"), 1)
                        for u in range(G):
                            for name in ("pq_ready_a", "pq_ready_b"):
                                pe.wait_ge(s(name), QN // 2 * min(u + 3, G))
                            if u >= 2:
                                pe.wait_ge(s("mc_ready"), 2 * QN * (u - 1))

                            def own(q, row, bank, h, m):
                                lo, ci, pos = HN * (h % 2), h // 2, (CH * q, CH * q)
                                o = bank[row, h * HN:(h + 1) * HN]
                                pe.matmul(o, at[row, m[0], m[1], 1, :], pq[row, u, h, HN:2 * HN], start=True, stop=False, tile_position=pos)
                                pe.matmul(o, at[row, m[0], m[1], 3, :], tok[row, u, h * HN:(h + 1) * HN], start=False, stop=True, tile_position=pos)
                                return pe.matmul(bank[lo:lo + HN, D + ci * CH:D + (ci + 1) * CH], pq[row, u, h, 0:HN], at[row, m[0], m[1], 1, :],
                                                 start=True, stop=True, tile_position=(CH * q, lo))

                            each(u, own).then_inc(s("own_made"), 1)
                            pe.wait_ge(s("own_ready"), 2 * QN * (u + 1))

                            def maps(q, row, bank, h, m):
                                lo, ci, pos = HN * (h % 2), h // 2, (CH * q, HN * (h % 2))
                                pe.matmul(bank[lo:lo + HN, ci * HN:(ci + 1) * HN], pq[row, u, h, 0:HN], tm[row, u, 1, h * HN:(h + 1) * HN],
                                          start=True, stop=True, tile_position=pos)
                                o = bank[lo:lo + HN, P + ci * HN:P + (ci + 1) * HN]
                                pe.matmul(o, tm[row, u, 1, h * HN:(h + 1) * HN], pq[row, u, h, HN:2 * HN], start=True, stop=False, tile_position=pos)
                                return pe.matmul(o, tm[row, u, 2, h * HN:(h + 1) * HN], tok[row, u, h * HN:(h + 1) * HN], start=False, stop=True,
                                                 tile_position=pos)

                            each(u, maps).then_inc(s("mc_made"), 1)
                        pe.wait_ge(s("mc_ready"), 2 * QN * G)
                        for t in range(NCH):
                            u, q = t // QN, t % QN
                            pe.wait_ge(s("st_ready"), 2 * t + 1)
                            for par in range(2):
                                lo = HN * par
                                for i in range(DC):
                                    mm = pe.matmul(ps[6 + par][lo:lo + HN, i * HN:(i + 1) * HN], mt[lo:lo + HN, u, i, q, :], st[lo:lo + HN, t, i, :],
                                                   start=True, stop=True, tile_position=(lo, lo))
                            mm.then_inc(s("st_made"), 1)
                        for u in range(G):
                            if u >= 2:
                                pe.wait_ge(s("ys_ready"), 2 * (u - 1))
                            for par in range(2):
                                lo = HN * par
                                for i in range(DC):
                                    for q in range(QN):
                                        mm = pe.matmul(ps[2 * (u % 2) + par][CH * q:CH * (q + 1), i * HN:(i + 1) * HN],
                                                       rp[lo:lo + HN, u, i, CH * q:CH * (q + 1)], st[lo:lo + HN, QN * u + q, i, :],
                                                       start=True, stop=True, tile_position=(lo, CH * q))
                            mm.then_inc(s("ys_made"), 1)
                        pe.wait_ge(s("gated"), 1)
                        for k in range(DC):
                            for u in range(G):
                                pe.transpose(ps[4 + k][:, u * P:(u + 1) * P], y[:, u, k * P:(k + 1) * P], c["ident"][:, :]).then_inc(s("y_turned"), 1)
                        pe.wait_ge(s("yt_ready"), DC)
                        for u in range(G):
                            for k in range(DC):
                                mm = pe.matmul(ps[u // 2][:, (u % 2) * D:(u % 2 + 1) * D], yt[:, k, u * P:(u + 1) * P], w_o[:, k, :],
                                               start=k == 0, stop=k == DC - 1)
                            if u % 2:
                                mm.then_inc(s("out_made"), 1)

                    @block.vector
                    def _(dve):
                        flat = dd[:, :, :, :].rearrange("p a b n -> p (a b n)")
                        w = chn[:, 1, :, :].rearrange("p c n -> p (c n)")
                        dve.wait_ge(s("w_here"), 16)
                        for i in range(DC):
                            dve.tensor_tensor_scan(wc[:, i * GT:(i + 1) * GT], not_first[:, :], chn[:, 1, i, :], 0.0, ALU.mult, ALU.add).then_inc(s("wc_ready"), 1)
                        dve.wait_ge(s("wc_ready"), DC)
                        dve.tensor_tensor(flat[:, 0:2 * GT], wc[:, :], w, ALU.subtract).then_inc(s("ends_ready"), 1)
                        by_chunk = wc[:, :].rearrange("p (q n) -> p q n", n=CH)
                        dve.tensor_tensor(flat[:, 2 * GT:4 * GT].rearrange("p (q n) -> p q n", n=CH),
                                          by_chunk[:, :, CH - 1:CH].to_broadcast([P, DC * NCH, CH]), by_chunk, ALU.subtract).then_inc(s("ends_ready"), 1)
                        dve.wait_ge(s("end_exp"), 2)
                        dve.wait_ge(s("a_here"), 16)
                        dve.tensor_tensor(a_end, chn[:, 3, :, :], flat[:, 0:2 * GT].rearrange("p (c n) -> p c n", c=DC),
                                          ALU.mult).then_inc(s("a_end"), 1)
                        dve.wait_ge(s("r_here"), 16)
                        dve.tensor_tensor(rt[:, :, :], chn[:, 0, :, :], flat[:, 4 * GT:6 * GT].rearrange("p (c n) -> p c n", c=DC),
                                          ALU.mult).then_inc(s("a_end"), 1)
                        dve.wait_ge(s("a_end"), 2)
                        dve.wait_ge(s("bk_end"), 3)

                        def exponents(i):
                            n = LEVELS[i]
                            v = halves(wc[:, :], n)
                            whole = wc[:, :].rearrange("p (b m) -> p b m", m=2 * n)
                            out = dd[:, i % 2, :, :].rearrange("p a (b n) -> p a b n", n=n)
                            mid = v[:, :, 0, n - 1:n].to_broadcast([P, DC * GT // (2 * n), n])
                            if i >= 2:
                                dve.wait_ge(s("bk_ready"), 2 * (i - 1))
                                dve.wait_ge(s("ar_ready"), 2 * (i - 1))
                            dve.tensor_tensor(out[:, 0, :, :], mid, v[:, :, 0, :], ALU.subtract).then_inc(s("dd_ready"), 1)
                            dve.tensor_tensor(out[:, 1, :, :], v[:, :, 1, :], mid, ALU.subtract).then_inc(s("dd_ready"), 1)
                            dve.tensor_tensor(out[:, 2, :, :], whole[:, :, n - 1:2 * n - 1], mid, ALU.subtract).then_inc(s("dd_ready"), 1)

                        def scaled(i):
                            n = LEVELS[i]
                            dve.wait_ge(s("dd_exp"), i + 1)
                            if i == 1:
                                dve.wait_ge(s("tm_made"), G)
                            if i >= 2:
                                dve.wait_ge(s("level_made"), 2 * (i - 1))
                            for j, (src, e) in enumerate(((3, 2), (0, 1))):
                                dve.tensor_tensor(ar_s[i % 2][:, j, :, :].rearrange("p c n -> p (c n)").rearrange("p (b n) -> p b n", n=n),
                                                  halves(chn[:, src, :, :].rearrange("p c n -> p (c n)"), n)[:, :, 1, :],
                                                  dd[:, i % 2, e, :].rearrange("p (b n) -> p b n", n=n), ALU.mult).then_inc(s("ar_ready"), 1)

                        exponents(0)
                        exponents(1)
                        scaled(0)
                        for i in range(len(LEVELS) + 1):
                            if i + 1 < len(LEVELS):
                                scaled(i + 1)
                            if i + 2 < len(LEVELS):
                                exponents(i + 2)
                            for par in range(2):
                                dve.wait_ge(s("level_made"), 2 * i + par + 1)
                                if i:
                                    dve.wait_ge(s("at_ready"), 2 * i + par - 1)
                                bank = ps[(2 * i + par) % 8]
                                if i < len(LEVELS):
                                    m = LEVELS[i]
                                    late = halves(masks[i][:, :], m)[:, :, 1, :]
                                    out = at[:, par, :, :, :].rearrange("p v a n -> p (v a) n")
                                    if m == CH // 2:
                                        dve.copy_predicated(out[:, :, m:CH], wide(masks[i][:, m:CH], G * DC * 4),
                                                            bank[:, :].rearrange("p (a n) -> p a n", n=m)).then_inc(s("at_ready"), 1)
                                    else:
                                        dve.copy_predicated(out.rearrange("p a (b h n) -> p a b h n", h=2, n=m)[:, :, :, 1, :],
                                                            late.unsqueeze(1).to_broadcast([P, G * DC * 4, CH // (2 * m), m]),
                                                            bank[:, :].rearrange("p (a b n) -> p a b n", b=CH // (2 * m), n=m)
                                                            ).then_inc(s("at_ready"), 1)
                                else:
                                    dve.copy_predicated(at[:, par, :, :, :].rearrange("p v (a k) n -> p (v a) k n", k=2)[:, :, 1, :],
                                                        wide(masks[i][:, :], 2 * G * DC),
                                                        bank[:, :].rearrange("p (a n) -> p a n", n=CH)).then_inc(s("at_ready"), 1)
                        dve.wait_ge(s("at_ready"), 2 * (len(LEVELS) + 1))
                        for u in range(G):
                            for par in range(2):
                                dve.transpose(bai[:, u, 1, par::2, :], at[:, par, DC * u:DC * (u + 1), 0, :]).then_inc(s("turned_ready"), 1)
                        for u in range(G):
                            dve.tensor_tensor(bai[:, u, 2, :, :].rearrange("p (c r) n -> p c r n", r=2),
                                              at[:, :, DC * u:DC * (u + 1), 0, :].rearrange("p r c n -> p c r n"),
                                              eye[:, :].unsqueeze(1).unsqueeze(1).to_broadcast([P, DC, 2, CH]), ALU.add).then_inc(s("inv_ready"), 1)
                        for step in range(5):
                            for u in range(G):
                                dve.wait_ge(s("fill_made"), G * step + u + 1)
                                if step == 0:
                                    dve.wait_ge(s("inv_ready"), G)
                                for q in range(0 if step else QN // 2, QN):
                                    row, bank = slice(CH * q, CH * (q + 1)), ps[4 * (u % 2) + q]
                                    lo = POWERS_FROM[step]
                                    if lo < 2:
                                        dve.tensor_copy(bai[row, u, lo:2, :, :].rearrange("p a h n -> p (a h n)"), bank[row, P * lo:2 * P]
                                                        ).then_inc(s("fill_read_b"), 1)
                                    if step == 0:
                                        dve.tensor_copy(xq[row, u, :, :].rearrange("p h n -> p (h n)"), bank[row, 2 * P:4 * P]
                                                        ).then_inc(s("fill_read_b"), 1)
                                    else:
                                        inverse = bai[row, u, 2, :, :].rearrange("p h n -> p (h n)")
                                        dve.tensor_tensor(inverse, inverse, bank[row, 2 * P:3 * P], ALU.add).then_inc(s("fill_read_b"), 1)
                        for u in range(G):
                            dve.wait_ge(s("pq_made"), u + 1)
                            for q in range(QN // 2, QN):
                                row = slice(CH * q, CH * (q + 1))
                                dve.tensor_copy(pq[row, u, :, :].rearrange("p h n -> p (h n)"), ps[4 * (u % 2) + q][row, :]).then_inc(s("pq_ready_b"), 1)
                        for u in range(G):
                            dve.wait_ge(s("own_made"), u + 1)
                            for q in range(QN):
                                row, bank = slice(CH * q, CH * (q + 1)), ps[4 * (u % 2) + q]
                                dve.tensor_copy(y[row, u, :], bank[row, 0:D]).then_inc(s("own_ready"), 1)
                                cut = slice(u * P + CH * q, u * P + CH * (q + 1))
                                dve.tensor_tensor(rp[:, u, :, CH * q:CH * (q + 1)], bank[:, D:D + DC * CH].rearrange("p (c n) -> p c n", c=DC),
                                                  rt[:, :, cut], ALU.add).then_inc(s("own_ready"), 1)
                            dve.wait_ge(s("mc_made"), u + 1)
                            dve.wait_ge(s("dg_ready"), DC * (u + 1))
                            for q in range(QN):
                                bank = ps[4 * (u % 2) + q]
                                dve.tensor_tensor(mt[:, u, :, q, :], bank[:, 0:P].rearrange("p (c n) -> p c n", c=DC), dg[:, u, q::QN, :],
                                                  ALU.add).then_inc(s("mc_ready"), 1)
                                dve.tensor_copy(cc[:, u, :, q, :], bank[:, P:2 * P].rearrange("p (c n) -> p c n", c=DC)).then_inc(s("mc_ready"), 1)
                        dve.tensor_copy(st[:, 0, :, :], st[:, NCH, :, :]).then_inc(s("st_ready"), 1)
                        dve.wait_ge(s("st_ready"), 1)
                        dve.wait_ge(s("mc_ready"), 2 * QN * G)
                        for t in range(NCH):
                            u, q = t // QN, t % QN
                            dve.wait_ge(s("st_made"), t + 1)
                            for par in range(2):
                                lo = HN * par
                                dve.tensor_tensor(st[lo:lo + HN, t + 1, :, :], ps[6 + par][lo:lo + HN, 0:P].rearrange("p (c n) -> p c n", c=DC),
                                                  cc[lo:lo + HN, u, :, q, :], ALU.add).then_inc(s("st_ready"), 1)
                        dve.wait_ge(s("own_ready"), 2 * QN * G)
                        for u in range(G):
                            dve.wait_ge(s("ys_made"), u + 1)
                            for par in range(2):
                                part = y[:, u, :].rearrange("p (c h n) -> p c h n", c=DC, h=2)[:, :, par, :]
                                dve.tensor_tensor(part, part, ps[2 * (u % 2) + par][:, 0:P].rearrange("p (c n) -> p c n", c=DC), ALU.add).then_inc(s("ys_ready"), 1)
                        dve.wait_ge(s("ys_ready"), 2 * G)
                        for k in range(G * HEADS):
                            dve.bn_stats(stats[:, k, :], y[:, k // HEADS, (k % HEADS) * HN:(k % HEADS + 1) * HN]).then_inc(s("stats_ready"), 1)
                        for k in range(G * HEADS):
                            dve.wait_ge(s("stats_ready"), k + 1)
                            dve.bn_aggr(mv[:, k, :], stats[:, k, :]).then_inc(s("mv_ready"), 1)
                        dve.wait_ge(s("mv_ready"), G * HEADS)
                        dve.tensor_scalar(var[:, :], mv[:, :, 1], 0.00064, None, ALU.add).then_inc(s("var_ready"), 1)
                        dve.wait_ge(s("rstd_ready"), 1)
                        for k in range(G * HEADS):
                            part = y[:, k // HEADS, (k % HEADS) * HN:(k % HEADS + 1) * HN]
                            dve.tensor_scalar(part, part, mv[:, k, 0:1], rstd[:, k:k + 1], ALU.subtract, ALU.mult).then_inc(s("normed"), 1)
                        dve.wait_ge(s("normed"), G * HEADS)
                        dve.tensor_tensor(y[:, :, :], y[:, :, :], wide(lnw[:, :], G), ALU.mult).then_inc(s("tail"), 1)
                        for u in range(G):
                            v = tok[:, u, 0:D].rearrange("p (h n) -> p h n", h=HEADS)
                            dve.tensor_tensor(v, v, tok[:, u, 2 * D:TOK].unsqueeze(2).to_broadcast([P, HEADS, HN]), ALU.mult).then_inc(s("bonus_v"), 1)
                        dve.wait_ge(s("tail"), 1)
                        dve.tensor_tensor(y[:, :, :], y[:, :, :], wide(lnb[:, :], G), ALU.add).then_inc(s("tail"), 1)
                        dve.wait_ge(s("tail"), 2)
                        dve.wait_ge(s("bonus_v"), G)
                        dve.tensor_tensor(y[:, :, :], y[:, :, :], tok[:, :, 0:D], ALU.add).then_inc(s("tail"), 1)
                        dve.wait_ge(s("tail"), 3)
                        dve.tensor_tensor(y[:, :, :], y[:, :, :], tok[:, :, D:2 * D], ALU.mult).then_inc(s("gated"), 1)
                        dve.wait_ge(s("x1_here"), 16)
                        for h in range(2):
                            dve.wait_ge(s("out_made"), h + 1)
                            dve.tensor_tensor(x1[:, 2 * h:2 * h + 2, :], ps[h][:, :].rearrange("p (g n) -> p g n", g=2), x1[:, 2 * h:2 * h + 2, :],
                                              ALU.add).then_inc(s("out_ready"), 1)


QH = AH // 4
VW = 32
QT = S // P
OH = P // AD
PARTS = ((0, 0), (0, 1), (1, 0), (0, 2), (2, 0), (1, 1))
KR = AD * len(PARTS)


def normalise(dve, s, x, out, stats, mv, var, rstd, gain, shift):
    for u in range(G):
        dve.bn_stats(stats[:, u, :], x[:, u, :]).then_inc(s("stats_ready"), 1)
    for u in range(G):
        dve.wait_ge(s("stats_ready"), u + 1)
        dve.bn_aggr(mv[:, u, :], stats[:, u, :]).then_inc(s("mv_ready"), 1)
    dve.wait_ge(s("mv_ready"), G)
    dve.tensor_scalar(var[:, :], mv[:, :, 1], 1e-5, None, ALU.add).then_inc(s("var_ready"), 1)
    dve.wait_ge(s("rstd_ready"), 1)
    for u in range(G):
        dve.tensor_scalar(out[:, u, :], x[:, u, :], mv[:, u, 0:1], rstd[:, u:u + 1], ALU.subtract, ALU.mult).then_inc(s("centred"), 1)
    dve.wait_ge(s("centred"), G)
    dve.tensor_tensor(out[:, :, :], out[:, :, :], wide(gain[:, :], G), ALU.mult).then_inc(s("scaled"), 1)
    dve.wait_ge(s("scaled"), 1)
    dve.tensor_tensor(out[:, :, :], out[:, :, :], wide(shift[:, :], G), ALU.add).then_inc(s("h_ready"), 1)


def row_of(io, name):
    return io[name].rearrange("(a n) -> a n", a=1).to_broadcast([P, D])


def attention_inputs(pr, io, c):
    nc = pr.nc
    with ExitStack() as ctx:
        def sb(name, shape):
            return ctx.enter_context(nc.sbuf_tensor("h_" + name, shape, F32))

        ps = [ctx.enter_context(nc.psum_tensor(f"h_bank{i}", [P, 512], F32)) for i in range(8)]
        w = sb("w", [P, DC, 3 * D])
        gain, shift = sb("gain", [P, D]), sb("shift", [P, D])
        cos, sin = sb("cos", [P, QT, AD // 2]), sb("sin", [P, QT, AD // 2])
        x, h = sb("x", [P, G, D]), sb("h", [P, G, D])
        stats, mv, var, rstd = sb("stats", [P, G, 6]), sb("mv", [P, G, 2]), sb("var", [P, G]), sb("rstd", [P, G])
        ht = sb("ht", [P, DC, GT])
        qk = sb("qk", [P, G, 2 * D])
        t1, t2 = sb("t1", [P, G, 2 * AH, AD // 2]), sb("t2", [P, G, 2 * AH, AD // 2])
        t3, t4 = sb("t3", [P, G, 2 * AH, AD // 2]), sb("t4", [P, G, 2 * AH, AD // 2])
        slots = sb("slots", [P, G, 2, AH, AD])
        parts = ctx.enter_context(nc.sbuf_tensor("h_parts", [P, 2, 2, 3, GT], BF16))
        rest = sb("rest", [P, 4, GT])
        v = sb("v", [P, G, AH, VW])
        with pr.body() as (block, s):
            @block.sync
            def _(sp):
                sp.dma_start(w[:, :, :], io["L1_ffn_Wqkv_P"].rearrange("(c p) n -> p c n", p=P)).then_inc(s("w_here"), 16)
                sp.dma_start(gain[:, :], row_of(io, "L1_ffn_ln1_g")).then_inc(s("w_here"), 16)
                sp.dma_start(shift[:, :], row_of(io, "L1_ffn_ln1_b")).then_inc(s("w_here"), 16)
                sp.dma_start(cos[:, :, :], io["cos"].rearrange("(u p) n -> p u n", p=P)).then_inc(s("w_here"), 16)
                sp.dma_start(sin[:, :, :], io["sin"].rearrange("(u p) n -> p u n", p=P)).then_inc(s("w_here"), 16)
                sp.wait_ge(s("w_here"), 80)

            @block.gpsimd
            def _(pool):
                pool.memset(v[:, :, :, AD:VW], 0.0).then_inc(s("zeroed"), 1)
                pool.wait_ge(s("zeroed"), 1)
                pool.memset(v[:, :, :, AD:AD + 1], 1.0)
        with nc.Fori(0, B) as b:
            for half in range(S // GT):
                with pr.body() as (block, s):
                    @block.sync
                    def _(sp):
                        sp.dma_start(x[:, :, :], rows(io["s_xn"], b * (S // GT) + half, GT)).then_inc(s("x_here"), 16)
                        sp.wait_ge(s("v_ready"), G)
                        for a in range(QH):
                            sp.dma_start(io["s_v2"][bass.ds(b * QH * S + a * S + half * GT, GT), :].rearrange("(u p) c -> p u c", p=P),
                                         v[:, :, 4 * a:4 * a + 4, :].rearrange("p u h n -> p u (h n)")).then_inc(s("stored"), 16)
                        for j, out in enumerate((io["s_qt"], io["s_kt"])):
                            for o in range(2):
                                sp.wait_ge(s("low_ready"), 2 * j + o + 1)
                                sp.dma_start(out[bass.ds((b * 2 + o) * 3 * P, 3 * P), half * GT:(half + 1) * GT].rearrange("(a p) n -> p a n", p=P),
                                             parts[:, j, o, :, :]).then_inc(s("stored"), 16)
                        sp.wait_ge(s("stored"), 16 * (QH + 4))

                    @block.gpsimd
                    def _(pool):
                        pool.wait_ge(s("var_ready"), 1)
                        pool.tensor_tensor(rstd[:, :], var[:, :], c["minus_half"][:, 0:G], ALU.pow).then_inc(s("rstd_ready"), 1)
                        for u in range(G):
                            pool.wait_ge(s("qk_ready"), u + 1)
                            one = qk[:, u, :].rearrange("p (h n) -> p h n", n=AD)
                            pool.tensor_tensor(t3[:, u, :, :], one[:, :, 0:8], wide(sin[:, G * half + u, :], 2 * AH), ALU.mult).then_inc(s("t_ready_b"), 1)
                            pool.tensor_tensor(t4[:, u, :, :], one[:, :, 8:16], wide(cos[:, G * half + u, :], 2 * AH), ALU.mult).then_inc(s("t_ready_b"), 1)

                    @block.scalar
                    def _(act):
                        for k in range(DC):
                            act.wait_ge(s("h_turned"), G * (k + 1))
                            act.activation(ht[:, k, :], ps[k][:, :], ACT.Copy).then_inc(s("ht_ready"), 1)
                        for u in range(G):
                            act.wait_ge(s("qkv_made"), u + 1)
                            act.activation(qk[:, u, :], ps[2 + 2 * (u % 2)][:, :], ACT.Copy).then_inc(s("qk_ready"), 1)
                            act.activation(v[:, u, :, 0:AD], ps[3 + 2 * (u % 2)][:, 0:D].rearrange("p (h n) -> p h n", n=AD), ACT.Copy).then_inc(s("v_ready"), 1)
                        for i in range(4):
                            act.wait_ge(s("slots_turned"), i + 1)
                            act.activation(parts[:, i // 2, i % 2, 0, :], ps[(6, 7, 0, 1)[i]][:, :], ACT.Copy).then_inc(s("high_ready"), 1)
                        for i in range(4):
                            act.wait_ge(s("rest_ready"), i + 1)
                            act.activation(parts[:, i // 2, i % 2, 1, :], rest[:, i, :], ACT.Copy).then_inc(s("mid_ready"), 1)

                    @block.tensor
                    def _(pe):
                        pe.wait_ge(s("h_ready"), 1)
                        for k in range(DC):
                            for u in range(G):
                                pe.transpose(ps[k][:, u * P:(u + 1) * P], h[:, u, k * P:(k + 1) * P], c["ident"][:, :]).then_inc(s("h_turned"), 1)
                        pe.wait_ge(s("ht_ready"), DC)
                        for u in range(G):
                            if u >= 2:
                                pe.wait_ge(s("v_ready"), u - 1)
                            for k in range(DC):
                                pe.matmul(ps[2 + 2 * (u % 2)][:, :], ht[:, k, u * P:(u + 1) * P], w[:, k, 0:2 * D], start=k == 0, stop=k == DC - 1)
                            for k in range(DC):
                                mm = pe.matmul(ps[3 + 2 * (u % 2)][:, 0:D], ht[:, k, u * P:(u + 1) * P], w[:, k, 2 * D:3 * D], start=k == 0, stop=k == DC - 1)
                            mm.then_inc(s("qkv_made"), 1)
                        pe.wait_ge(s("slots_ready"), 4 * G)
                        for i in range(4):
                            for u in range(G):
                                mm = pe.transpose(ps[(6, 7, 0, 1)[i]][:, u * P:(u + 1) * P],
                                                  slots[:, u, i // 2, OH * (i % 2):OH * (i % 2 + 1), :].rearrange("p h n -> p (h n)"), c["ident"][:, :])
                            mm.then_inc(s("slots_turned"), 1)

                    @block.vector
                    def _(dve):
                        dve.wait_ge(s("x_here"), 16)
                        normalise(dve, s, x, h, stats, mv, var, rstd, gain, shift)
                        for u in range(G):
                            dve.wait_ge(s("qk_ready"), u + 1)
                            one = qk[:, u, :].rearrange("p (h n) -> p h n", n=AD)
                            dve.tensor_tensor(t1[:, u, :, :], one[:, :, 0:8], wide(cos[:, G * half + u, :], 2 * AH), ALU.mult).then_inc(s("t_ready_a"), 1)
                            dve.tensor_tensor(t2[:, u, :, :], one[:, :, 8:16], wide(sin[:, G * half + u, :], 2 * AH), ALU.mult).then_inc(s("t_ready_a"), 1)
                            dve.wait_ge(s("t_ready_a"), 2 * (u + 1))
                            dve.tensor_tensor(t1[:, u, :, :], t1[:, u, :, :], t2[:, u, :, :], ALU.subtract).then_inc(s("rotated"), 1)
                            dve.wait_ge(s("t_ready_b"), 2 * (u + 1))
                            dve.tensor_tensor(t3[:, u, :, :], t3[:, u, :, :], t4[:, u, :, :], ALU.add).then_inc(s("rotated"), 1)
                            dve.wait_ge(s("rotated"), 2 * (u + 1))
                            for lo, t in ((0, t1), (8, t3)):
                                dve.tensor_scalar(slots[:, u, 0, :, lo:lo + 8], t[:, u, 0:AH, :], AD ** -0.5, None, ALU.mult).then_inc(s("slots_ready"), 1)
                                dve.tensor_copy(slots[:, u, 1, :, lo:lo + 8], t[:, u, AH:2 * AH, :]).then_inc(s("slots_ready"), 1)
                        for i in range(4):
                            dve.wait_ge(s("high_ready"), i + 1)
                            dve.tensor_tensor(rest[:, i, :], ps[(6, 7, 0, 1)[i]][:, :], parts[:, i // 2, i % 2, 0, :], ALU.subtract).then_inc(s("rest_ready"), 1)
                        for i in range(4):
                            dve.wait_ge(s("mid_ready"), i + 1)
                            dve.tensor_tensor(parts[:, i // 2, i % 2, 2, :], rest[:, i, :], parts[:, i // 2, i % 2, 1, :], ALU.subtract).then_inc(s("low_ready"), 1)


def row_units():
    return [(i, k, min(512, (i + 1) * P - 512 * k)) for i in range(QT) for k in range(i // 4 + 1)]


def softmax_attention(pr, io, c):
    nc = pr.nc
    with ExitStack() as ctx:
        def sb(name, shape):
            return ctx.enter_context(nc.sbuf_tensor("m_" + name, shape, F32))

        ps = ctx.enter_context(nc.psum_tensor("m_banks", [P, 8, 512], F32))
        qts = [ctx.enter_context(nc.sbuf_tensor(f"m_qt{w}", [KR + 3, 4, S], BF16)) for w in range(2)]
        kts = [ctx.enter_context(nc.sbuf_tensor(f"m_kt{w}", [KR + 3, 4, S], BF16)) for w in range(2)]
        ident = ctx.enter_context(nc.sbuf_tensor("m_ident", [P, P], BF16))
        vs = [sb(f"v{w}", [P, QT, 4, VW]) for w in range(2)]
        late = sb("late", [P, P])
        later = sb("later", [P, P])
        diag = sb("diag", [P, 2, 2, P])
        part = sb("part", [P, QT, 4, 3])
        top = sb("top", [P, QT, 4])
        rest = sb("rest", [P, QT, 4])
        tops = ctx.enter_context(nc.sbuf_tensor("m_tops", [P, QT, 4, 3], BF16))
        pt = sb("pt", [P, 2, QT, 2, 512])
        ot = sb("ot", [P, 2, 512])
        den = sb("den", [P, 2, 4, 4, 1])
        o = sb("o", [P, QT, 4, AD])
        with pr.body() as (block, s):
            @block.gpsimd
            def _(pool):
                pool.memset(part[:, :, :, :], -3.0e38)
                pool.memset(late[:, :], 0.0).then_inc(s("zeroed"), 1)
                pool.memset(later[:, :], 0.0).then_inc(s("zeroed"), 1)
                pool.wait_ge(s("zeroed"), 2)
                pool.affine_select(out=late[:, :], in_=late[:, :], compare_op=ALU.is_ge, fill=-3.0e38, base=0,
                                   pattern=[[-1, P]], channel_multiplier=1)
                pool.affine_select(out=later[:, :], in_=later[:, :], compare_op=ALU.is_ge, fill=-3.0e38, base=0,
                                   pattern=[[1, P]], channel_multiplier=-1)

            @block.vector
            def _(dve):
                dve.tensor_copy(ident[:, :], c["ident"][:, :])
                for kt in kts:
                    dve.memset(kt[KR:KR + 3, :, :], 1.0)
        units = [(i, k, wd, pair) for (i, k, wd) in row_units() for pair in range(2)]
        turns = [(span, pair, j, max(0, j * P - 512 * span)) for span in range(2) for pair in range(2) for j in range(4 * (span + 1))]
        with nc.Fori(0, B * 2) as octet:
            for w in range(2):
                n = octet * 2 + w
                qt, kt, v = qts[w], kts[w], vs[w]
                with pr.body() as (block, s):
                    @block.sync
                    def _(sp):
                        if w == 0:
                            for i in range(2):
                                for t, part in enumerate(PARTS):
                                    for j, (name, stack) in enumerate((("s_qt", qts[i]), ("s_kt", kts[i]))):
                                        sp.dma_start(stack[AD * t:AD * (t + 1), :, :],
                                                     io[name][bass.ds(octet * 3 * P + i * (P // 2) + part[j] * P, P // 2), :].rearrange("(h n) c -> n h c", n=AD)
                                                     ).then_inc(s(f"q_here{i}"), 16)
                                sp.dma_start(vs[i][:, :, :, :].rearrange("p u h n -> p u (h n)"),
                                             io["s_v2"][bass.ds((octet * 2 + i) * S, S), :].rearrange("(u p) c -> p u c", p=P)).then_inc(s(f"v_here{i}"), 16)
                            sp.wait_ge(s("q_here1"), 32 * len(PARTS))
                            sp.wait_ge(s("v_here1"), 16)
                        sp.wait_ge(s("o_ready"), 2)
                        sp.dma_start(io["s_o2"][bass.ds(n * S, S), :].rearrange("(u p) c -> p u c", p=P),
                                     o[:, :, :, :].rearrange("p u h n -> p u (h n)")).then_inc(s("stored"), 16)
                        sp.wait_ge(s("stored"), 16)

                    @block.tensor
                    def _(pe):
                        if w == 0:
                            pe.wait_ge(s("q_here0"), 32 * len(PARTS))
                        for m, (i, k, wd, pair) in enumerate(units):
                            if m >= 4:
                                pe.wait_ge(s("unit_read"), m - 3)
                            for h in range(2):
                                mm = pe.matmul(ps[:, 2 * (m % 4) + h, 0:wd], qt[0:KR, 2 * pair + h, i * P:(i + 1) * P],
                                               kt[0:KR, 2 * pair + h, 512 * k:512 * k + wd], start=True, stop=True)
                            mm.then_inc(s("unit_made"), 1)
                        pe.wait_ge(s("tops_ready"), 1)
                        pe.wait_ge(s("unit_read"), len(units))
                        for h in range(4):
                            for i in range(QT):
                                mm = pe.matmul(ps[KR:KR + 3, 2 * h + i // 4, (i % 4) * P:(i % 4 + 1) * P], tops[:, i, h, :], ident[:, :],
                                               start=True, stop=True, tile_position=(0, KR))
                            mm.then_inc(s("tops_turned"), 1)
                        pe.wait_ge(s("shifted"), 2)
                        pe.wait_ge(s("shifted_b"), 2)
                        if w == 0:
                            pe.wait_ge(s("v_here0"), 16)

                        def values(m):
                            span, pair, j, q0 = turns[m]
                            pe.wait_ge(s("exp_ready"), m + 1)
                            for h in range(2):
                                lo = VW * (2 * pair + h)
                                mm = pe.matmul(ps[lo:lo + VW, 6 + span, q0:512], v[:, j, 2 * pair + h, :], pt[:, (2 * span + pair) % 2, j, h, q0:512],
                                               start=j == 0, stop=j == 4 * span + 3, tile_position=(0, lo))
                            mm.then_inc(s("o_made"), 1)

                        def turned_back(span):
                            pe.wait_ge(s("ot_ready"), span + 1)
                            for i in range(4):
                                mm = pe.transpose(ps[:, 6 + span, i * P:(i + 1) * P], ot[:, span, i * P:(i + 1) * P], c["ident"][:, :])
                            mm.then_inc(s("o_turned"), 1)

                        LAG = 3
                        for m, (span, pair, j, q0) in enumerate(turns):
                            if m >= 3:
                                pe.wait_ge(s("exp_ready"), m - 2)
                            for h in range(2):
                                mm = pe.matmul(ps[:, 2 * (m % 3) + h, 0:512 - q0], kt[:, 2 * pair + h, j * P:(j + 1) * P],
                                               qt[:, 2 * pair + h, 512 * span + q0:512 * (span + 1)], start=True, stop=True)
                            mm.then_inc(s("turn_made"), 1)
                            if m >= LAG:
                                values(m - LAG)
                            if (span, pair, j) == (1, 0, 7):
                                turned_back(0)
                        for m in range(len(turns) - LAG, len(turns)):
                            values(m)
                        turned_back(1)

                    @block.scalar
                    def _(act):
                        for h in range(2):
                            act.wait_ge(s("tops_turned"), h + 1)
                            act.activation(qt[KR:KR + 3, h, :].rearrange("p (a n) -> p a n", a=2), ps[KR:KR + 3, 2 * h:2 * h + 2, :], ACT.Copy
                                           ).then_inc(s("shifted_b"), 1)
                        for m, (span, pair, j, q0) in enumerate(turns):
                            g = 2 * span + pair
                            if g >= 2:
                                act.wait_ge(s("o_made"), 4 if g == 2 else 8)
                            act.wait_ge(s("turn_made"), m + 1)
                            if j >= 4 * span:
                                act.wait_ge(s("hidden"), 4 * g + j - 4 * span + 1)
                            act.activation(pt[:, g % 2, j, :, q0:512], ps[:, 2 * (m % 3):2 * (m % 3) + 2, 0:512 - q0], ACT.Exp).then_inc(s("exp_ready"), 1)

                    @block.vector
                    def _(dve):
                        nd, nr = 0, 0
                        for m, (i, k, wd, pair) in enumerate(units):
                            dve.wait_ge(s("unit_made"), m + 1)
                            bank = ps[:, 2 * (m % 4):2 * (m % 4) + 2, :]
                            last = k == i // 4
                            w0 = wd - P if last else wd
                            if last:
                                if nd >= 2:
                                    dve.wait_ge(s("part_ready"), nd - 1)
                                ins = dve.tensor_tensor(diag[:, nd % 2, :, :], bank[:, :, w0:wd], wide(late[:, :], 2), ALU.add)
                                if w0 == 0:
                                    ins.then_inc(s("unit_read"), 1)
                                else:
                                    ins.then_inc(s("diag_ready"), 1)
                                    nr += 1
                            if w0:
                                dve.tensor_reduce(part[:, i, 2 * pair:2 * pair + 2, k], bank[:, :, 0:w0], AX.X, ALU.max).then_inc(s("unit_read"), 1)
                            if last:
                                if w0 == 0:
                                    dve.wait_ge(s("unit_read"), m + 1)
                                else:
                                    dve.wait_ge(s("diag_ready"), nr)
                                dve.tensor_reduce(part[:, i, 2 * pair:2 * pair + 2, 2], diag[:, nd % 2, :, :], AX.X, ALU.max).then_inc(s("part_ready"), 1)
                                nd += 1
                        dve.wait_ge(s("part_ready"), nd)
                        dve.wait_ge(s("unit_read"), len(units))
                        dve.tensor_reduce(top[:, :, :], part[:, :, :, :], AX.X, ALU.max).then_inc(s("top_ready"), 1)
                        dve.wait_ge(s("top_ready"), 1)
                        dve.tensor_scalar(rest[:, :, :], top[:, :, :], -1.0, None, ALU.mult).then_inc(s("top_ready"), 1)
                        for i in range(3):
                            dve.wait_ge(s("top_ready"), 2 + 2 * i)
                            part_ = dve.tensor_copy(tops[:, :, :, i], rest[:, :, :])
                            if i == 2:
                                part_.then_inc(s("tops_ready"), 1)
                                break
                            part_.then_inc(s("top_ready"), 1)
                            dve.wait_ge(s("top_ready"), 3 + 2 * i)
                            dve.tensor_tensor(rest[:, :, :], rest[:, :, :], tops[:, :, :, i], ALU.subtract).then_inc(s("top_ready"), 1)
                        for h in range(2, 4):
                            dve.wait_ge(s("tops_turned"), h + 1)
                            dve.tensor_copy(qt[KR:KR + 3, h, :].rearrange("p (a n) -> p a n", a=2), ps[KR:KR + 3, 2 * h:2 * h + 2, :]
                                            ).then_inc(s("shifted"), 1)

                        def copied(span):
                            dve.wait_ge(s("o_made"), (8, len(turns))[span])
                            dve.tensor_copy(ot[:, span, :], ps[:, 6 + span, :]).then_inc(s("ot_ready"), 1)

                        def normalised(span):
                            dve.wait_ge(s("o_turned"), span + 1)
                            out = ps[:, 6 + span, :].rearrange("p (i h n) -> p i h n", i=4, h=4)
                            dve.reciprocal(den[:, span, :, :, :], out[:, :, :, AD:AD + 1]).then_inc(s("den_ready"), 1)
                            dve.wait_ge(s("den_ready"), span + 1)
                            dve.tensor_tensor(o[:, 4 * span:4 * span + 4, :, :], out[:, :, :, 0:AD],
                                              den[:, span, :, :, :].to_broadcast([P, 4, 4, AD]), ALU.mult).then_inc(s("o_ready"), 1)

                        for m, (span, pair, j, q0) in enumerate(turns):
                            if j >= 4 * span:
                                dve.wait_ge(s("turn_made"), m + 1)
                                block_ = ps[:, 2 * (m % 3):2 * (m % 3) + 2, 0:P]
                                dve.tensor_tensor(block_, block_, wide(later[:, :], 2), ALU.add).then_inc(s("hidden"), 1)
                            if (span, pair, j) == (1, 0, 4):
                                copied(0)
                            if (span, pair, j) == (1, 1, 4):
                                normalised(0)
                        copied(1)
                        normalised(1)


NT = N // P
EO = E * CAP


def projection(pr, io, c):
    nc = pr.nc
    with ExitStack() as ctx:
        def sb(name, shape):
            return ctx.enter_context(nc.sbuf_tensor("p_" + name, shape, F32))

        ps = [ctx.enter_context(nc.psum_tensor(f"p_bank{i}", [P, 512], F32)) for i in range(8)]
        w, wg = sb("w", [P, DC, D]), sb("wg", [P, DC, E])
        gain, shift = sb("gain", [P, D]), sb("shift", [P, D])
        o, xn, rw = sb("o", [P, G, D]), sb("xn", [P, G, D]), sb("rw", [P, G, D])
        ot, ft = sb("ot", [P, DC, GT]), sb("ft", [P, DC, GT])
        flat = sb("flat", [P, G, D])
        lg = sb("lg", [P, G, E])
        ZR = EO // (N // GT)
        zero = sb("zero", [P, ZR // P, D])
        stats, mv, var, rstd = sb("stats", [P, G, 6]), sb("mv", [P, G, 2]), sb("var", [P, G]), sb("rstd", [P, G])
        with pr.body() as (block, s):
            @block.sync
            def _(sp):
                sp.dma_start(w[:, :, :], io["L1_ffn_Wproj"].rearrange("(c p) n -> p c n", p=P)).then_inc(s("w_here"), 16)
                sp.dma_start(wg[:, :, :], io["L1_ffn_Wgate"].rearrange("(c p) n -> p c n", p=P)).then_inc(s("w_here"), 16)
                sp.dma_start(gain[:, :], row_of(io, "L1_ffn_ln2_g")).then_inc(s("w_here"), 16)
                sp.dma_start(shift[:, :], row_of(io, "L1_ffn_ln2_b")).then_inc(s("w_here"), 16)
                sp.wait_ge(s("w_here"), 64)

            @block.gpsimd
            def _(pool):
                pool.memset(zero[:, :, :], 0.0)
        with nc.Fori(0, B) as b:
            for half in range(S // GT):
                with pr.body() as (block, s):
                    n = b * (S // GT) + half

                    @block.sync
                    def _(sp):
                        for a in range(QH):
                            sp.dma_start(o[:, :, 64 * a:64 * (a + 1)],
                                         io["s_o2"][bass.ds(b * QH * S + a * S + half * GT, GT), :].rearrange("(u p) c -> p u c", p=P)
                                         ).then_inc(s("o_here"), 16)
                        sp.dma_start(xn[:, :, :], rows(io["s_xn"], n, GT)).then_inc(s("xn_here"), 16)
                        sp.dma_start(rw[:, :, :], rows(io["s_rw"], n, GT)).then_inc(s("rw_here"), 16)
                        sp.dma_start(rows(io["s_ei"], n, ZR), zero[:, :, :]).then_inc(s("zeros_stored"), 16)
                        sp.wait_ge(s("base_ready"), 1)
                        sp.dma_start(rows(io["s_base"], n, GT), rw[:, :, :]).then_inc(s("stored"), 16)
                        sp.wait_ge(s("h_ready"), 1)
                        sp.dma_start(rows(io["s_flat"], n, GT), flat[:, :, :]).then_inc(s("stored"), 16)
                        sp.wait_ge(s("lg_ready"), 1)
                        sp.dma_start(rows(io["s_lg"], n, GT), lg[:, :, :]).then_inc(s("stored"), 16)
                        sp.wait_ge(s("stored"), 48)
                        sp.wait_ge(s("zeros_stored"), 16)

                    @block.gpsimd
                    def _(pool):
                        pool.wait_ge(s("var_ready"), 1)
                        pool.tensor_tensor(rstd[:, :], var[:, :], c["minus_half"][:, 0:G], ALU.pow).then_inc(s("rstd_ready"), 1)
                        pool.wait_ge(s("rw_here"), 16)
                        pool.wait_ge(s("x2_ready"), 2)
                        pool.tensor_tensor(rw[:, :, :], rw[:, :, :], xn[:, :, :], ALU.add).then_inc(s("base_ready"), 1)

                    @block.scalar
                    def _(act):
                        for k in range(DC):
                            act.wait_ge(s("o_turned"), k + 1)
                            act.activation(ot[:, k, :], ps[k][:, :], ACT.Copy).then_inc(s("ot_ready"), 1)
                        for k in range(DC):
                            act.wait_ge(s("f_turned"), k + 1)
                            act.activation(ft[:, k, :], ps[4 + k][:, :], ACT.Copy).then_inc(s("ft_ready"), 1)
                        act.wait_ge(s("lg_made"), 1)
                        act.activation(lg[:, :, :], ps[6][:, 0:G * E].rearrange("p (u e) -> p u e", u=G), ACT.Copy).then_inc(s("lg_ready"), 1)

                    @block.tensor
                    def _(pe):
                        pe.wait_ge(s("o_here"), 16 * QH)
                        for k in range(DC):
                            for u in range(G):
                                mm = pe.transpose(ps[k][:, u * P:(u + 1) * P], o[:, u, k * P:(k + 1) * P], c["ident"][:, :])
                            mm.then_inc(s("o_turned"), 1)
                        pe.wait_ge(s("ot_ready"), DC)
                        for u in range(G):
                            for k in range(DC):
                                mm = pe.matmul(ps[2 + u // 2][:, (u % 2) * D:(u % 2 + 1) * D], ot[:, k, u * P:(u + 1) * P], w[:, k, :],
                                               start=k == 0, stop=k == DC - 1)
                            if u % 2:
                                mm.then_inc(s("y_made"), 1)
                        pe.wait_ge(s("h_ready"), 1)
                        for k in range(DC):
                            for u in range(G):
                                mm = pe.transpose(ps[4 + k][:, u * P:(u + 1) * P], flat[:, u, k * P:(k + 1) * P], c["ident"][:, :])
                            mm.then_inc(s("f_turned"), 1)
                        pe.wait_ge(s("ft_ready"), DC)
                        for u in range(G):
                            for k in range(DC):
                                mm = pe.matmul(ps[6][:, u * E:(u + 1) * E], ft[:, k, u * P:(u + 1) * P], wg[:, k, :], start=k == 0, stop=k == DC - 1)
                        mm.then_inc(s("lg_made"), 1)

                    @block.vector
                    def _(dve):
                        dve.wait_ge(s("xn_here"), 16)
                        for h in range(2):
                            dve.wait_ge(s("y_made"), h + 1)
                            two = xn[:, 2 * h:2 * h + 2, :]
                            dve.tensor_tensor(two, two, ps[2 + h][:, :].rearrange("p (g n) -> p g n", g=2), ALU.add).then_inc(s("x2_ready"), 1)
                        dve.wait_ge(s("x2_ready"), 2)
                        normalise(dve, s, xn, flat, stats, mv, var, rstd, gain, shift)


def routing(pr, io, c, slot, gate, slot_in):
    nc = pr.nc
    with ExitStack() as ctx:
        def sb(name, shape, dtype=F32):
            return ctx.enter_context(nc.sbuf_tensor("r_" + name, shape, dtype))

        ps = ctx.enter_context(nc.psum_tensor("r_banks", [P, 2, 512], F32))
        lg, g = sb("lg", [P, NT, E]), sb("g", [P, NT, E])
        top, total = sb("top", [P, NT, 1]), sb("total", [P, NT, 1])
        rank, cmp = sb("rank", [P, NT, E]), sb("cmp", [P, 2, NT, E])
        mask, inner, tiles = sb("mask", [P, NT, E]), sb("inner", [P, NT, E]), sb("tiles", [P, NT, E])
        ahead = sb("ahead", [P, NT, E])
        keep, slots, picked = sb("keep", [P, NT, E]), sb("slots", [P, NT, E]), sb("picked", [P, NT, E])
        first, spare = sb("first", [P, E]), sb("spare", [P, 2, NT])
        f = sb("f", [P, 3, 2, NT])
        with pr.body() as (block, s):
            @block.gpsimd
            def _(pool):
                pool.iota(first[:, :], [[CAP, E]], base=0, channel_multiplier=0, allow_small_or_imprecise_dtypes=True).then_inc(s("made"), 1)
                pool.iota(spare[:, :, :], [[NT * P, 2], [P, NT]], base=EO, channel_multiplier=1, allow_small_or_imprecise_dtypes=True).then_inc(s("made"), 1)

            @block.sync
            def _(sp):
                sp.dma_start(lg[:, :, :], io["s_lg"].rearrange("(u p) e -> p u e", p=P)).then_inc(s("lg_here"), 16)

            @block.scalar
            def _(act):
                act.wait_ge(s("shifted"), 1)
                act.activation(g[:, :, :], lg[:, :, :], ACT.Exp).then_inc(s("exp_ready"), 1)

            @block.tensor
            def _(pe):
                pe.wait_ge(s("mask_ready"), 1)
                flat = mask[:, :, :].rearrange("p u e -> p (u e)")
                pe.matmul(ps[:, 0, 0:NT * E], c["upper"][:, :], flat, start=True, stop=True).then_inc(s("counted"), 1)
                pe.matmul(ps[:, 1, 0:NT * E], c["ones"][:, :], flat, start=True, stop=True).then_inc(s("counted"), 1)

            @block.vector
            def _(dve):
                steps = [0]

                def step(ins):
                    ins.then_inc(s("step"), 1)
                    steps[0] += 1
                    dve.wait_ge(s("step"), steps[0])

                def over(t):
                    return t[:, :, :].to_broadcast([P, NT, E])

                dve.wait_ge(s("lg_here"), 16)
                step(dve.tensor_reduce(top[:, :, 0], lg[:, :, :], AX.X, ALU.max))
                dve.tensor_tensor(lg[:, :, :], lg[:, :, :], over(top), ALU.subtract).then_inc(s("shifted"), 1)
                dve.wait_ge(s("exp_ready"), 1)
                step(dve.tensor_reduce(total[:, :, 0], g[:, :, :], AX.X, ALU.add))
                step(dve.reciprocal(total[:, :, :], total[:, :, :]))
                step(dve.tensor_tensor(g[:, :, :], g[:, :, :], over(total), ALU.mult))
                step(dve.scalar_tensor_tensor(g[:, :, :], g[:, :, :], 2.0 ** -126, g[:, :, :], ALU.is_ge, ALU.mult))
                step(dve.memset(rank[:, :, :], 0.0))
                for e in range(E):
                    other = g[:, :, e:e + 1]
                    if e < E - 1:
                        mine = g[:, :, e + 1:E]
                        step(dve.tensor_tensor(cmp[:, 0, :, e + 1:E], mine, other.to_broadcast([P, NT, E - 1 - e]), ALU.is_le))
                        step(dve.tensor_tensor(rank[:, :, e + 1:E], rank[:, :, e + 1:E], cmp[:, 0, :, e + 1:E], ALU.add))
                    if e:
                        mine = g[:, :, 0:e]
                        step(dve.tensor_tensor(cmp[:, 1, :, 0:e], mine, other.to_broadcast([P, NT, e]), ALU.is_lt))
                        step(dve.tensor_tensor(rank[:, :, 0:e], rank[:, :, 0:e], cmp[:, 1, :, 0:e], ALU.add))
                dve.tensor_scalar(mask[:, :, :], rank[:, :, :], 2.0, None, ALU.is_lt).then_inc(s("mask_ready"), 1)
                dve.wait_ge(s("counted"), 2)
                step(dve.tensor_copy(inner[:, :, :], ps[:, 0, 0:NT * E].rearrange("p (u e) -> p u e", e=E)))
                step(dve.tensor_copy(tiles[:, :, :], ps[:, 1, 0:NT * E].rearrange("p (u e) -> p u e", e=E)))
                step(dve.memset(ahead[:, 0, :], 0.0))
                for u in range(1, NT):
                    step(dve.tensor_tensor(ahead[:, u, :], ahead[:, u - 1, :], tiles[:, u - 1, :], ALU.add))
                step(dve.tensor_tensor(inner[:, :, :], inner[:, :, :], ahead[:, :, :], ALU.add))
                step(dve.tensor_scalar(inner[:, :, :], inner[:, :, :], -1.0, None, ALU.add))
                step(dve.tensor_scalar(keep[:, :, :], inner[:, :, :], float(CAP), None, ALU.is_lt))
                step(dve.tensor_scalar(slots[:, :, :], inner[:, :, :], float(CAP - 1), 0.0, ALU.min, ALU.max))
                dve.wait_ge(s("made"), 2)
                step(dve.tensor_tensor(slots[:, :, :], slots[:, :, :], wide(first[:, :], NT), ALU.add))
                step(dve.tensor_tensor(g[:, :, :], g[:, :, :], keep[:, :, :], ALU.mult))
                for k in range(2):
                    for i, t in enumerate((slots, g, keep)):
                        step(dve.scalar_tensor_tensor(picked[:, :, :], rank[:, :, :], float(k), t[:, :, :], ALU.is_equal, ALU.mult))
                        step(dve.tensor_reduce(f[:, i, k, :], picked[:, :, :], AX.X, ALU.add))
                step(dve.tensor_copy(slot[:, :, :], f[:, 0, :, :]))
                step(dve.tensor_copy(gate[:, :, :], f[:, 1, :, :]))
                step(dve.tensor_tensor(f[:, 0, :, :], f[:, 0, :, :], spare[:, :, :], ALU.subtract))
                step(dve.tensor_tensor(f[:, 0, :, :], f[:, 0, :, :], f[:, 2, :, :], ALU.mult))
                step(dve.tensor_tensor(f[:, 0, :, :], f[:, 0, :, :], spare[:, :, :], ALU.add))
                step(dve.tensor_copy(slot_in[:, :, :], f[:, 0, :, :]))


def dispatch(pr, io, c, slot_in):
    nc = pr.nc
    with ExitStack() as ctx:
        flat = ctx.enter_context(nc.sbuf_tensor("d_flat", [P, NT, D], F32))
        scattered = ctx.enter_context(nc.semaphore("scattered"))
        with pr.body() as (block, s):
            @block.gpsimd
            def _(pool):
                for u in range(NT):
                    if u % 8 == 0:
                        pool.wait_ge(s("flat_here"), 2 * (u + 8))
                    for k in range(2):
                        pool.indirect_dma_start(out=io["s_ei"], out_offset=bass.IndirectOffsetOnAxis(ap=slot_in[:, k, u:u + 1], axis=0),
                                                in_=flat[:, u, :], in_offset=None).then_inc(scattered, 16)
                pool.wait_ge(scattered, 32 * NT)

            @block.scalar
            def _(act):
                for u in range(0, NT, 8):
                    act.dma_start(flat[:, u:u + 8, :], io["s_flat"][u * P:(u + 8) * P, :].rearrange("(u p) c -> p u c", p=P)).then_inc(s("flat_here"), 16)
                    act.wait_ge(s("flat_here"), 2 * (u + 8))


def combine(pr, io, c, slot, gate, out):
    nc = pr.nc
    W = 8
    with ExitStack() as ctx:
        base = ctx.enter_context(nc.sbuf_tensor("c_base", [P, 2, W, D], F32))
        y = ctx.enter_context(nc.sbuf_tensor("c_y", [P, 2, 2, W, D], F32))
        R = NT // W
        gathered = [ctx.enter_context(nc.semaphore(f"gathered{i}")) for i in range(2)]
        with pr.body() as (block, s):
            @block.gpsimd
            def _(pool):
                for r in range(R):
                    if r >= 2:
                        pool.wait_ge(s("summed"), W * (r - 1))
                    for u in range(W):
                        for k in range(2):
                            pool.indirect_dma_start(out=y[:, r % 2, k, u, :], out_offset=None, in_=io["s_eo"],
                                                    in_offset=bass.IndirectOffsetOnAxis(ap=slot[:, k, W * r + u:W * r + u + 1], axis=0)
                                                    ).then_inc(gathered[r % 2], 16)

            @block.sync
            def _(sp):
                for r in range(R):
                    if r >= 2:
                        sp.wait_ge(s(f"stored{r % 2}"), 16 * (r // 2))
                    sp.dma_start(base[:, r % 2, :, :], io["s_base"][r * W * P:(r + 1) * W * P, :].rearrange("(u p) c -> p u c", p=P)
                                 ).then_inc(s(f"base_here{r % 2}"), 16)

            @block.scalar
            def _(act):
                for r in range(R):
                    act.wait_ge(s("summed"), W * (r + 1))
                    act.dma_start(out[r * W * P:(r + 1) * W * P, :].rearrange("(u p) c -> p u c", p=P), base[:, r % 2, :, :]).then_inc(s(f"stored{r % 2}"), 16)
                for i in range(min(2, R)):
                    act.wait_ge(s(f"stored{i}"), 16 * ((R + 1 - i) // 2))

            @block.vector
            def _(dve):
                for r in range(R):
                    dve.wait_ge(s(f"base_here{r % 2}"), 16 * (r // 2 + 1))
                    dve.wait_ge(gathered[r % 2], 32 * W * (r // 2 + 1))
                    for k in range(2):
                        if k:
                            dve.wait_ge(s("first_added"), W * (r + 1))
                        for u in range(W):
                            one = base[:, r % 2, u, :]
                            dve.scalar_tensor_tensor(one, y[:, r % 2, k, u, :], gate[:, k, W * r + u:W * r + u + 1], one, ALU.mult,
                                                     ALU.add).then_inc(s("summed" if k else "first_added"), 1)


def program(nc, io):
    with ExitStack() as ctx:
        def sb(name, shape, dtype=F32):
            return ctx.enter_context(nc.sbuf_tensor(name, shape, dtype))

        pr = Program(nc, ctx)
        c = constants(pr, sb, io)
        layer0_attention(pr, io, c)
        layer0_feed_forward(pr, io, c)
        recurrence_inputs(pr, io, c)
        recurrence(pr, io, c)
        attention_inputs(pr, io, c)
        softmax_attention(pr, io, c)
        projection(pr, io, c)
        slot, gate, slot_in = sb("slot", [P, 2, NT], U32), sb("gate", [P, 2, NT]), sb("slot_in", [P, 2, NT], U32)
        routing(pr, io, c, slot, gate, slot_in)
        dispatch(pr, io, c, slot_in)
        experts(pr, io, c)
        combine(pr, io, c, slot, gate, io["out"])


SCRATCH = {
    "s_a": (N, D), "s_xs": (N, D), "s_x1": (N, D), "s_xn": (N, D),
    "s_ch": (2 * B * P, CHN * DC * GT), "s_tok": (2 * B * P, 4 * TOK), "s_rw": (N, D),
    "s_qt": (B * 6 * P, S), "s_kt": (B * 6 * P, S), "s_v2": (B * QH * S, 4 * VW), "s_o2": (B * QH * S, 4 * AD),
    "s_base": (N, D), "s_flat": (N, D), "s_lg": (N, E), "s_ei": (EO + 2 * N, D), "s_eo": (EO, D),
}


def laid_out(inputs):
    d = {}
    for name, a in inputs.items():
        a = np.asarray(a)
        if name == "L0_attn_x":
            d[name] = a.reshape(N, D)
        elif name in ("L0_attn_Wq", "L0_attn_Wk", "L0_attn_Wv", "L0_attn_Wo", "L0_ffn_w_up", "L0_ffn_w_down",
                      "L1_attn_w_receptance", "L1_attn_w_key", "L1_attn_w_value", "L1_attn_w_output"):
            d[name + "_T"] = a.T
        elif name in ["L1_attn_" + n for n in COLS]:
            pass
        elif name == "L1_attn_time_maa_w2":
            d[name] = a.reshape(-1, D)
        elif name == "L1_ffn_Wqkv":
            d[name + "_P"] = a.reshape(D, AH, 3, AD).transpose(0, 2, 1, 3).reshape(D, 3 * D)
        elif name == "L1_ffn_W1":
            d[name] = a.reshape(E * D, FF)
        elif name == "L1_ffn_W2":
            d[name] = a.reshape(E * FF, D)
        elif name == "L1_ffn_b1":
            d[name + "_T"] = a.reshape(E, FC, P).transpose(0, 2, 1).reshape(E * P, FC)
        elif name in ("L1_attn_ln_w", "L1_attn_ln_b"):
            d[name] = a.reshape(D)
        else:
            d[name] = a
    d["L1_attn_columns"] = np.stack([np.asarray(inputs["L1_attn_" + n]).reshape(DC, P) for n in COLS]).transpose(2, 0, 1).reshape(P, -1)
    inv = (1.0 / np.float32(10000.0) ** (np.arange(0, AD, 2, dtype=np.float32) / np.float32(AD))).astype(np.float32)
    angle = np.arange(S, dtype=np.float32)[:, None] * inv
    d["cos"], d["sin"] = np.cos(angle), np.sin(angle)
    return {name: np.ascontiguousarray(a) for name, a in d.items()}


def kernel(**inputs):
    import concourse.bacc as bacc
    from concourse.bass_utils import run_bass_kernel_spmd

    nc = bacc.Bacc("TRN2", target_bir_lowering=False, num_devices=1)
    arrays = laid_out(inputs)
    io = {name: nc.dram_tensor(name, a.shape, mybir.dt.from_np(a.dtype), kind="ExternalInput").ap() for name, a in arrays.items()}
    for name, shape in SCRATCH.items():
        io[name] = nc.dram_tensor(name, shape, BF16 if name in ("s_qt", "s_kt") else F32, kind="Internal").ap()
    io["out"] = nc.dram_tensor("out", (N, D), F32, kind="ExternalOutput").ap()
    program(nc, io)
    r = run_bass_kernel_spmd(nc, [arrays], core_ids=[0])
    return r.results[0]["out"].reshape(B, S, D)
```
